# Optimizing a Trainium2 kernel written in Bass

```python
import numpy as np
import jax
import jax.numpy as jnp

def _softmax(x, axis=-1):
    return jax.nn.softmax(x, axis=axis)

def _gelu(x):
    return jax.nn.gelu(x, approximate=True)

def _silu(x):
    return jax.nn.silu(x)

def _sigmoid(x):
    return jax.nn.sigmoid(x)

def _layernorm(x, axis=-1, eps=1e-05):
    m = jnp.mean(x, axis=axis, keepdims=True)
    v = jnp.var(x, axis=axis, keepdims=True)
    return (x - m) / jnp.sqrt(v + eps)

def _scatter_add(tgt, idx, src, axis=0):
    return tgt.at[idx].add(src)

def _segment_sum(src, seg, n):
    return jax.ops.segment_sum(src, seg, n)
kernel_name = 'mk_cond_resid_d4_seqx_r4_10edf6'

def setup_inputs(seed: int=0):
    np.random.seed(seed)
    _w = jnp.asarray

    def _rec_inputs():
        import jax
        import jax.numpy as jnp
        _rk = jax.random.key(seed)
        x = -0.003407 + 1.001 * jax.random.normal(jax.random.fold_in(_rk, 1), (32, 64, 512), jnp.float32)
        _lenS = 64 - jax.random.randint(jax.random.fold_in(_rk, 7), (32,), 0, max(1, 64 // 4) + 1, jnp.int32)
        _lenS2 = 64 - jax.random.randint(jax.random.fold_in(_rk, 8), (32,), 0, max(1, 64 // 4) + 1, jnp.int32)
        itok_Bx257_0_4111 = jax.random.randint(jax.random.fold_in(_rk, 11), (32, 257), 0, 1028, jnp.int32)
        itok_B_37_3939 = jax.random.randint(jax.random.fold_in(_rk, 12), (32,), 37, 985, jnp.int32)
        itok_B_0_7 = jax.random.randint(jax.random.fold_in(_rk, 13), (32,), 0, 8, jnp.int32)
        itok_B_0_3 = jax.random.randint(jax.random.fold_in(_rk, 14), (32,), 0, 4, jnp.int32)
        itok_B_0_6 = jax.random.randint(jax.random.fold_in(_rk, 15), (32,), 0, 7, jnp.int32)
        return (x, itok_Bx257_0_4111, itok_B_37_3939, itok_B_0_7, itok_B_0_3, itok_B_0_6)
    x, itok_Bx257_0_4111, itok_B_37_3939, itok_B_0_7, itok_B_0_3, itok_B_0_6 = _rec_inputs()

    def _L0_cond_setup():
        import jax, jax.numpy as jnp
        import numpy as np
        H, G, HD = (8, 4, 64)
        GSZ = H // G
        BLOCK = 16
        WINDOW = 256
        SCALE = 256.0 ** (-0.5)
        EPS = 1e-06
        THETA = 10000.0
        B, T, D = (16, 4, 512)
        NBLK = 257

        def _rms(x, scale):
            var = jnp.mean(x * x, axis=-1, keepdims=True)
            return x * jax.lax.rsqrt(var + EPS) * (1.0 + scale)

        def _rope(x, pos):
            half = HD // 2
            inv = 1.0 / THETA ** (jnp.arange(half, dtype=jnp.float32) / half)
            ang = pos[:, :, None].astype(jnp.float32) * inv
            cos = jnp.cos(ang)[:, None, :, :]
            sin = jnp.sin(ang)[:, None, :, :]
            x1, x2 = (x[..., :half], x[..., half:])
            return jnp.concatenate([x1 * cos - x2 * sin, x2 * cos + x1 * sin], axis=-1)
        key = jax.random.key(seed)
        ks = jax.random.split(key, 10)
        inv_d = 1.0 / np.sqrt(D)
        return {'x': jax.random.normal(ks[0], (B, T, D), jnp.float32), 'Wq': jax.random.normal(ks[1], (H * HD, D), jnp.float32) * inv_d, 'Wk': jax.random.normal(ks[2], (G * HD, D), jnp.float32) * inv_d, 'Wv': jax.random.normal(ks[3], (G * HD, D), jnp.float32) * inv_d, 'Wo': jax.random.normal(ks[4], (D, H * HD), jnp.float32) * inv_d, 'q_norm_scale': jax.random.normal(ks[5], (HD,), jnp.float32) * 0.02, 'k_norm_scale': jax.random.normal(ks[6], (HD,), jnp.float32) * 0.02, 'k_blocks': jax.random.normal(ks[7], (B * NBLK, G, BLOCK, HD), jnp.float32), 'v_blocks': jax.random.normal(ks[8], (B * NBLK, G, BLOCK, HD), jnp.float32), 'block_tables': jnp.arange(B * NBLK, dtype=jnp.int32).reshape(B, NBLK), 'kv_lens': jax.random.randint(ks[9], (B,), 0, 1024, dtype=jnp.int32)}
    _L0_cond_all = _L0_cond_setup()
    _L0_cond_in = {k: v for k, v in _L0_cond_all.items() if k in ('Wq', 'Wk', 'Wv', 'Wo', 'q_norm_scale', 'k_norm_scale', 'k_blocks', 'v_blocks')}
    del _L0_cond_all

    def _L1_cond_setup():
        import jax, jax.numpy as jnp
        import numpy as np
        B, C, D, T, N_SUBJECTS = (128, 64, 64, 512, 8)
        key = jax.random.key(seed)
        kx, ks, kw = jax.random.split(key, 3)
        x = jax.random.normal(kx, (B, C, T), dtype=jnp.float32)
        subjects = jax.random.randint(ks, (B,), 0, N_SUBJECTS, dtype=jnp.int64)
        weights = jax.random.normal(kw, (N_SUBJECTS, C, D), dtype=jnp.float32) * (1.0 / C ** 0.5)
        return {'x': x, 'subjects': subjects, 'weights': weights}
    _L1_cond_all = _L1_cond_setup()
    _L1_cond_in = {k: v for k, v in _L1_cond_all.items() if k in ('weights',)}
    del _L1_cond_all

    def _L2_cond_setup():
        import jax, jax.numpy as jnp
        import numpy as np
        B, S, D_IN, D_OUT, R, E = (8, 512, 512, 512, 16, 4)
        key = jax.random.key(seed)
        ks = jax.random.split(key, 7)
        x = jax.random.normal(ks[0], (B, S, D_IN), dtype=jnp.float32)
        W_base = jax.random.normal(ks[1], (D_OUT, D_IN), dtype=jnp.float32) * 0.02
        Wt = jax.random.normal(ks[2], (D_IN, D_IN), dtype=jnp.float32) * 0.02
        A = jax.random.normal(ks[3], (E, R, D_IN), dtype=jnp.float32) * 0.02
        B_w = jax.random.normal(ks[4], (E, D_OUT, R), dtype=jnp.float32) * 0.02
        Wp = jax.random.normal(ks[5], (D_OUT, D_OUT), dtype=jnp.float32) * 0.02
        scaling = jnp.ones((E,), dtype=jnp.float32)
        adapter_idx = jax.random.randint(ks[6], (B,), 0, E)
        return {'x': x, 'W_base': W_base, 'Wt': Wt, 'A': A, 'B_w': B_w, 'Wp': Wp, 'scaling': scaling, 'adapter_idx': adapter_idx}
    _L2_cond_all = _L2_cond_setup()
    _L2_cond_in = {k: v for k, v in _L2_cond_all.items() if k in ('W_base', 'Wt', 'A', 'B_w', 'Wp', 'scaling')}
    del _L2_cond_all

    def _L3_cond_setup():
        import jax, jax.numpy as jnp
        import numpy as np
        B, T, D_IN, D_OUT = (16, 512, 512, 512)
        N_ADAPTERS, RANK = (8, 16)
        key = jax.random.key(seed)
        k_x, k_w, k_a, k_b, k_s, k_idx = jax.random.split(key, 6)
        x = jax.random.normal(k_x, (B, T, D_IN), dtype=jnp.float32)
        W = jax.random.normal(k_w, (D_OUT, D_IN), dtype=jnp.float32) * (1.0 / np.sqrt(D_IN))
        A = jax.random.normal(k_a, (N_ADAPTERS, RANK, D_IN), dtype=jnp.float32) * 0.02
        Bm = jax.random.normal(k_b, (N_ADAPTERS, D_OUT, RANK), dtype=jnp.float32) * 0.02
        scalings = jnp.ones((N_ADAPTERS,), dtype=jnp.float32)
        adapter_idx = jax.random.randint(k_idx, (B,), 0, N_ADAPTERS, dtype=jnp.int32)
        return {'x': x, 'W': W, 'A': A, 'Bm': Bm, 'scalings': scalings, 'adapter_idx': adapter_idx}
    _L3_cond_all = _L3_cond_setup()
    _L3_cond_in = {k: v for k, v in _L3_cond_all.items() if k in ('W', 'A', 'Bm', 'scalings')}
    del _L3_cond_all
    return {'x': x, 'itok_Bx257_0_4111': itok_Bx257_0_4111, 'itok_B_37_3939': itok_B_37_3939, 'itok_B_0_7': itok_B_0_7, 'itok_B_0_3': itok_B_0_3, 'itok_B_0_6': itok_B_0_6, 'L0_cond_Wq': _L0_cond_in['Wq'], 'L0_cond_Wk': _L0_cond_in['Wk'], 'L0_cond_Wv': _L0_cond_in['Wv'], 'L0_cond_Wo': _L0_cond_in['Wo'], 'L0_cond_q_norm_scale': _L0_cond_in['q_norm_scale'], 'L0_cond_k_norm_scale': _L0_cond_in['k_norm_scale'], 'L0_cond_k_blocks': _L0_cond_in['k_blocks'], 'L0_cond_v_blocks': _L0_cond_in['v_blocks'], 'L1_cond_weights': _L1_cond_in['weights'], 'L2_cond_W_base': _L2_cond_in['W_base'], 'L2_cond_Wt': _L2_cond_in['Wt'], 'L2_cond_A': _L2_cond_in['A'], 'L2_cond_B_w': _L2_cond_in['B_w'], 'L2_cond_Wp': _L2_cond_in['Wp'], 'L2_cond_scaling': _L2_cond_in['scaling'], 'L3_cond_W': _L3_cond_in['W'], 'L3_cond_A': _L3_cond_in['A'], 'L3_cond_Bm': _L3_cond_in['Bm'], 'L3_cond_scalings': _L3_cond_in['scalings']}

def reference(x, itok_Bx257_0_4111, itok_B_37_3939, itok_B_0_7, itok_B_0_3, itok_B_0_6, L0_cond_Wq, L0_cond_Wk, L0_cond_Wv, L0_cond_Wo, L0_cond_q_norm_scale, L0_cond_k_norm_scale, L0_cond_k_blocks, L0_cond_v_blocks, L1_cond_weights, L2_cond_W_base, L2_cond_Wt, L2_cond_A, L2_cond_B_w, L2_cond_Wp, L2_cond_scaling, L3_cond_W, L3_cond_A, L3_cond_Bm, L3_cond_scalings):
    import jax
    import jax.numpy as jnp

    def _L0_cond_ref(x, Wq, Wk, Wv, Wo, q_norm_scale, k_norm_scale, k_blocks, v_blocks, block_tables, kv_lens):
        import jax, jax.numpy as jnp
        import numpy as np
        H, G, HD = (8, 4, 64)
        GSZ = H // G
        BLOCK = 16
        WINDOW = 256
        SCALE = 256.0 ** (-0.5)
        EPS = 1e-06
        THETA = 10000.0
        B, T, D = (16, 4, 512)
        NBLK = 257

        def _rms(x, scale):
            var = jnp.mean(x * x, axis=-1, keepdims=True)
            return x * jax.lax.rsqrt(var + EPS) * (1.0 + scale)

        def _rope(x, pos):
            half = HD // 2
            inv = 1.0 / THETA ** (jnp.arange(half, dtype=jnp.float32) / half)
            ang = pos[:, :, None].astype(jnp.float32) * inv
            cos = jnp.cos(ang)[:, None, :, :]
            sin = jnp.sin(ang)[:, None, :, :]
            x1, x2 = (x[..., :half], x[..., half:])
            return jnp.concatenate([x1 * cos - x2 * sin, x2 * cos + x1 * sin], axis=-1)
        Bx, Tx, _ = x.shape
        q = jnp.einsum('btd,od->bto', x, Wq).reshape(Bx, Tx, H, HD).transpose(0, 2, 1, 3)
        k = jnp.einsum('btd,od->bto', x, Wk).reshape(Bx, Tx, G, HD).transpose(0, 2, 1, 3)
        v = jnp.einsum('btd,od->bto', x, Wv).reshape(Bx, Tx, G, HD).transpose(0, 2, 1, 3)
        q = _rms(q, q_norm_scale)
        k = _rms(k, k_norm_scale)
        pos = kv_lens[:, None] + jnp.arange(Tx, dtype=jnp.int32)
        q = _rope(q, pos)
        k = _rope(k, pos)
        slot = pos // BLOCK
        off = pos % BLOCK
        blk = jnp.take_along_axis(block_tables, slot, axis=1)
        k_blocks = k_blocks.at[blk, :, off, :].set(k.transpose(0, 2, 1, 3))
        v_blocks = v_blocks.at[blk, :, off, :].set(v.transpose(0, 2, 1, 3))
        k_all = k_blocks[block_tables].transpose(0, 2, 1, 3, 4).reshape(Bx, G, -1, HD)
        v_all = v_blocks[block_tables].transpose(0, 2, 1, 3, 4).reshape(Bx, G, -1, HD)
        S = k_all.shape[2]
        qg = q.reshape(Bx, G, GSZ, Tx, HD)
        scores = jnp.einsum('bghtd,bgsd->bghts', qg, k_all) * SCALE
        kpos = jnp.arange(S, dtype=jnp.int32)
        allowed = (kpos[None, None, :] <= pos[:, :, None]) & (kpos[None, None, :] > pos[:, :, None] - WINDOW)
        scores = jnp.where(allowed[:, None, None, :, :], scores, -jnp.inf)
        p = jax.nn.softmax(scores, axis=-1)
        o = jnp.einsum('bghts,bgsd->bghtd', p, v_all).reshape(Bx, H, Tx, HD)
        o = o.transpose(0, 2, 1, 3).reshape(Bx, Tx, H * HD)
        return jnp.einsum('bto,do->btd', o, Wo)

    def _L1_cond_ref(x, subjects, weights):
        import jax, jax.numpy as jnp
        import numpy as np
        B, C, D, T, N_SUBJECTS = (128, 64, 64, 512, 8)
        w = weights[subjects]
        out = jnp.einsum('bct,bcd->bdt', x, w)
        return out

    def _L2_cond_ref(x, W_base, Wt, A, B_w, Wp, scaling, adapter_idx):
        import jax, jax.numpy as jnp
        import numpy as np
        B, S, D_IN, D_OUT, R, E = (8, 512, 512, 512, 16, 4)
        base = jnp.einsum('bsi,oi->bso', x, W_base)
        h = jnp.einsum('bsi,ji->bsj', x, Wt)
        Ab = A[adapter_idx]
        Bb = B_w[adapter_idx]
        sc = scaling[adapter_idx]
        z = jnp.einsum('bsj,brj->bsr', h, Ab)
        l = jnp.einsum('bsr,bor->bso', z, Bb)
        lora_out = jnp.einsum('bso,po->bsp', l, Wp) * sc[:, None, None]
        return base + lora_out

    def _L3_cond_ref(x, W, A, Bm, scalings, adapter_idx):
        import jax, jax.numpy as jnp
        import numpy as np
        B, T, D_IN, D_OUT = (16, 512, 512, 512)
        N_ADAPTERS, RANK = (8, 16)
        H = jnp.einsum('btd,od->bto', x, W)
        A_b = A[adapter_idx]
        B_b = Bm[adapter_idx]
        s_b = scalings[adapter_idx]
        xa = jnp.einsum('btd,brd->btr', x, A_b)
        delta = jnp.einsum('btr,bor->bto', xa, B_b)
        delta = jax.lax.stop_gradient(delta * s_b[:, None, None])
        return H + delta
    x = x + _L0_cond_ref(x, L0_cond_Wq, L0_cond_Wk, L0_cond_Wv, L0_cond_Wo, L0_cond_q_norm_scale, L0_cond_k_norm_scale, L0_cond_k_blocks, L0_cond_v_blocks, itok_Bx257_0_4111, itok_B_37_3939)
    x = x + _L1_cond_ref(x, itok_B_0_7, L1_cond_weights)
    x = x + _L2_cond_ref(x, L2_cond_W_base, L2_cond_Wt, L2_cond_A, L2_cond_B_w, L2_cond_Wp, L2_cond_scaling, itok_B_0_3)
    x = x + _L3_cond_ref(x, L3_cond_W, L3_cond_A, L3_cond_Bm, L3_cond_scalings, itok_B_0_6)
    return x

_drawn_inputs = setup_inputs


def setup_inputs(seed=0):
    import zlib

    import numpy as np

    out = dict(_drawn_inputs(seed))
    spreads = {'L2_cond_scaling': (1.0, 0.6), 'L3_cond_scalings': (1.0, 0.6)}
    factors = {'L0_cond_Wk': 9.153,
     'L0_cond_q_norm_scale': 57.143,
     'L0_cond_k_norm_scale': 64.0,
     'L2_cond_Wt': 8.0,
     'L2_cond_A': 8.0,
     'L2_cond_B_w': 8.0,
     'L2_cond_Wp': 8.0,
     'L2_cond_W_base': 5.239}
    for name, (base, spread) in spreads.items():
        noise = np.random.default_rng([zlib.crc32(name.encode()), seed]).standard_normal(out[name].shape)
        drawn = base * np.exp(spread * noise) if base else spread * noise
        out[name] = jnp.asarray(drawn.astype(out[name].dtype))
    for name, factor in factors.items():
        out[name] = (out[name] * factor).astype(out[name].dtype)
    return out
```

```python
import concourse.bass as bass
from concourse import mybir
from contextlib import ExitStack
import numpy as np

NB, NT, D = 32, 64, 512
G, HD = 4, 64
BLOCK, WINDOW, NSLOT = 16, 256, 257
NPOOL = 16 * NSLOT
TILES = NB // 2
C = D // 128
WS = 21
NW = 5
WK = WS * BLOCK
CH = 3
KP = WK // CH
SP_ = KP // BLOCK
NE2, NE3, RANK = 4, 8, 16
NONE = 4096
NEG = 1.0e30

_WIDTHS = [("ident", 128), ("diff", WK), ("negc", WK), ("inv", 32), ("tpos", 1), ("e2", 1), ("e3", 1),
           ("slots", NSLOT), ("win", WS), ("order", NW * NW * NB), ("toff", NW * BLOCK), ("code", 1), ("off", 1),
           ("spread", SP_ * KP), ("ones", NB)]
CONST, _at = {}, 0
for _n, _w in _WIDTHS:
    CONST[_n] = (_at, _w)
    _at += _w
NCONST = _at


def constants():
    t = np.zeros((128, NCONST), np.float32)

    def put(name, a):
        c, w = CONST[name]
        t[:a.shape[0], c:c + w] = a.reshape(a.shape[0], w)

    p = np.arange(128)
    put("ident", np.eye(128))
    put("diff", np.arange(WK)[None, :] - (p % NT)[:, None])
    put("negc", np.broadcast_to(-10000.0 * np.arange(WK), (128, WK)))
    inv = np.float32(1.0) / (np.float32(10000.0) ** (np.arange(32, dtype=np.float32) / np.float32(32)))
    put("inv", np.broadcast_to(inv.astype(np.float32), (128, 32)))
    put("tpos", (p % NT)[:, None])
    put("e2", (p // RANK)[:, None])
    put("e3", (p // RANK)[:, None])
    put("slots", np.broadcast_to(np.arange(NSLOT), (NB, NSLOT)))
    put("win", np.broadcast_to(np.arange(WS) - (WS - NW), (NB, WS)))
    b = np.arange(NB)
    j = np.arange(NW)
    put("order", (NW * (b[:, None, None, None] - b[None, None, None, :]) + j[None, :, None, None] - j[None, None, :, None] > 0))
    put("toff", np.broadcast_to(np.arange(NW * BLOCK), (NB, NW * BLOCK)))
    put("code", (NT * b + 1)[:, None])
    put("off", np.arange(BLOCK)[:, None])
    q = np.arange(KP)
    put("spread", (q[None, None, :] == BLOCK * np.arange(SP_)[None, :, None] + np.arange(BLOCK)[:, None, None]))
    put("ones", np.ones((NB, NB)))
    return t


class Tile:

    def __init__(self, j, c):
        self.j, self.c = j, c

    def n(self, per, plus):
        return self.j * (2 * per) + (per * self.c + plus)

    def part(self, u):
        return 2 * self.c + u

    def b(self, u, per, plus):
        return self.j * (4 * per) + (per * self.part(u) + plus)

    def ring(self, u):
        q, r = divmod(self.part(u), 4)
        return r, self.j * 48 + 48 * (q + 1)


def after(eng, sem, value):
    if not isinstance(value, int) or value > 0:
        eng.wait_ge(sem, value)


def build(nc, xt, xtok, kvrows, wkv, wq, wo, qs, ks, w1, wb, wt, a2t, b2t, wpt, s2, w3, a3t, b3t, s3,
          table, kvl, subj, ad2, ad3, const, out):
    f32, i32 = mybir.dt.float32, mybir.dt.int32
    ALU, ACT, AX = mybir.AluOpType, mybir.ActivationFunctionType, mybir.AxisListType.X
    ctx = ExitStack()
    with ctx:
        def sb(name, shape, dt=f32):
            return ctx.enter_context(nc.sbuf_tensor(name, shape, dt))

        def sem(name):
            return ctx.enter_context(nc.semaphore(name))

        newkv = nc.dram_tensor("newkv", [NB * NT, 2 * G * HD], f32).ap()
        newkv_t = newkv.rearrange("(n p) f -> n p f", p=128)

        cst = sb("cst", [128, NCONST])

        def con(name, rows=128):
            c, w = CONST[name]
            return cst[0:rows, c:c + w]

        ident = con("ident")
        wkv_s = sb("wkv_s", [128, C, 512])
        wq_s = sb("wq_s", [128, C, 512])
        wo_s = sb("wo_s", [128, C, 512])
        wb_s = sb("wb_s", [128, C, 512])
        w3_s = sb("w3_s", [128, C, 512])
        wide = sb("wide", [128, 2, C, 512])
        wt_s, wpt_s = wide[:, 0], wide[:, 1]
        flat = wide[:].rearrange("p a c n -> p (a c n)")
        prob = [flat[:, G * WK * i:G * WK * (i + 1)].rearrange("p (g k) -> p g k", g=G) for i in range(2)]
        neg_s = flat[:, 2 * G * WK:3 * G * WK].rearrange("p (g k) -> p g k", g=G)
        windows = sb("windows", [128, 4 * CH * 512])
        kv_s = [windows[0:KP, CH * 512 * i:CH * 512 * (i + 1)].rearrange("p (c n) -> p c n", c=CH) for i in range(4)]
        same = windows[0:NB, 0:NW * WS * NB].rearrange("p (j n) -> p j n", j=NW)
        rows = windows[0:BLOCK, NW * WS * NB:(NW + 2) * WS * NB].rearrange("p (k n) -> p k n", k=2)
        a2_s = sb("a2_s", [128, C, 64])
        b2_s = sb("b2_s", [128, C, 64])
        a3_s = sb("a3_s", [128, C, 128])
        b3_s = sb("b3_s", [128, 512])
        down2 = sb("down2", [128, C, 64])
        up2 = sb("up2", [128, 512])
        scl2, scl3 = sb("scl2", [128, 1]), sb("scl3", [128, 1])
        idx2, idx3 = sb("idx2", [128, NB], i32), sb("idx3", [128, NB], i32)
        pick2, pick3 = sb("pick2", [128, NB]), sb("pick3", [128, NB])
        kvb = sb("kvb", [128, NB], i32)
        kvi = sb("kvi", [128, NB], i32)
        k0f, r0f = sb("k0f", [128, NB]), sb("r0f", [128, NB])
        band = sb("band", [128, NB])
        limit = sb("limit", [128, NB])
        start = sb("start", [128, NB])
        pos = sb("pos", [128, TILES])
        ang = sb("ang", [128, TILES, 32])
        turns = sb("turns", [128, TILES, 32])
        rest = sb("rest", [128, TILES, 32])
        sinx = sb("sinx", [128, TILES, 32])
        cosx = sb("cosx", [128, TILES, 32])
        nscale = {"q": sb("qscale", [128, 64]), "k": sb("kscale", [128, 64])}
        costab = {"q": sb("qcos", [128, TILES, 64]), "k": sb("kcos", [128, TILES, 64])}
        sintab = {"q": sb("qsin", [128, TILES, 64]), "k": sb("ksin", [128, TILES, 64])}
        tab_i = sb("tab_i", [NB, NSLOT], i32)
        tab_f = sb("tab_f", [NB, NSLOT])
        kvc = sb("kvc", [NB, 3], i32)
        kvcf = sb("kvcf", [NB, 2])
        want = sb("want", [NB, WS])
        hit = sb("hit", [NB, NSLOT])
        blk = sb("blk", [NB, WS])
        blkd = sb("blkd", [NB, WS, NB])
        blkrow = sb("blkrow", [NB, WS, NB])
        later = sb("later", [NB, NW, NW * NB])
        wt_tok = sb("wt_tok", [NB, NW * BLOCK])
        wt_ge = sb("wt_ge", [NB, NW * BLOCK])
        cover = sb("cover", [NB, NW * BLOCK])
        code = sb("code", [NB, NW * BLOCK])
        wins = sb("wins", [NB, NW * BLOCK])
        wcode = sb("wcode", [NB, NW * BLOCK])
        none = sb("none", [BLOCK, WS * NB])
        idx_all = sb("idx_all", [KP, NB, 2 * CH], i32)
        idx_b = [sb(f"idx_b{i}", [KP, 2 * CH], i32) for i in range(2)]
        xt_s = [sb(f"xt_s{i}", [128, C, 128]) for i in range(4)]
        kvo = [sb(f"kvo{i}", [128, 512]) for i in range(2)]
        nr = {}
        for w, h in (("q", 8), ("k", 4)):
            nr[w] = dict(sq=sb(w + "_sq", [128, h, 64]), ss=sb(w + "_ss", [128, h]), ms=sb(w + "_ms", [128, h]),
                         rstd=sb(w + "_rstd", [128, h]), n=sb(w + "_n", [128, h, 64]), t1=sb(w + "_t1", [128, h, 64]),
                         t2=sb(w + "_t2", [128, h, 64]))
        half = sb("half", [128, 8])
        kt_s = sb("kt_s", [128, 2, WK])
        qrot = sb("qrot", [128, 512])
        qz = sb("qz", [128, 2, 512])
        mask = [sb(f"mask{i}", [128, WK]) for i in range(2)]
        negmax = sb("negmax", [128, G])
        psum_p = [sb(f"psum_p{i}", [128, G]) for i in range(2)]
        rinv = [sb(f"rinv{i}", [128, G]) for i in range(2)]
        pt_s = [sb(f"pt_s{i}", [KP, CH, 128]) for i in range(G)]
        ot_s = sb("ot_s", [128, 4, 128])
        xtok_s = sb("xtok_s", [128, 512])
        x1 = sb("x1", [128, 512])
        w1raw = sb("w1raw", [128, 128])
        w1i = sb("w1i", [128, 128])
        x2t = sb("x2t", [128, C, 128])
        x3t = sb("x3t", [128, C, 128])
        z2m = sb("z2m", [128, 128])
        z3m = sb("z3m", [128, 128])
        xo = sb("xo", [128, 512])
        subj_s = sb("subj_s", [1, 2], i32)

        gb = [ctx.enter_context(nc.psum_tensor(f"gb{i}", [128, 512], f32)) for i in range(2)]
        sbk = [ctx.enter_context(nc.psum_tensor(f"sbk{i}", [128, 512], f32)) for i in range(2)]
        tb = [ctx.enter_context(nc.psum_tensor(f"tb{i}", [128, 512], f32)) for i in range(2)]
        ob = [ctx.enter_context(nc.psum_tensor(f"ob{i}", [128, 512], f32)) for i in range(2)]

        names = """l_const l_table l_kv l_scale l_wkv l_wq l_wo l_wb l_w3 l_up l_ad
            set_dve zeroed tab_ready sin_done
            blkd_ready blkrow_mm same_ready later_ready lose_mm wcode_ready win_mm rows_ready idx_mm idx_ready
            down_mm down_ev up_mm up_ev w_ident
            ka_mm ka_sq ka_ss ka_ms ka_rstd ka_n ka_t2 ka_rot ka_v
            q_mm q_sq q_ss q_ms q_rstd q_n q_t2 q_rot qt_mm qz_ready l_xq
            kt_mm kt_ev s_mm mask_band mask_start mask_ready negs_ready exp_done rinv_ready prob_ready
            pt_mm pt_ev pv_mm ot_ev idx_copied
            wo_mm x1_ready l_xtok l_subj l_w1 w1i_ready l1_mm x2_ready z2_mm z2_ready x3_mm x3_ready
            z3_mm z3_ready out_mm xo_ready stored""".split()
        S = {n: sem(n) for n in names}
        l_xt = [sem(f"l_xt{i}") for i in range(4)]
        kv_stored = [sem(f"kv_stored{i}") for i in range(2)]
        kv_old = [sem(f"kv_old{i}") for i in range(4)]
        kv_new = [sem(f"kv_new{i}") for i in range(4)]
        block = ctx.enter_context(nc.Block())

        def wait_alone(eng, *waits):
            waits = [(sem, v if isinstance(v, int) else eng.snap(eng.to_reg(v)))
                     for sem, v in waits if not isinstance(v, int) or v > 0]
            if waits:
                eng.wait_ge(S["l_const"], 16)
                for sem, v in waits:
                    eng.wait_ge(sem, v)

        HALF_A = TILES // 2

        @block.sync
        def _(sp):
            def load_xt(n, i):
                sp.dma_start(xt_s[i][:], xt[n]).then_inc(l_xt[i], 16)

            load_xt(0, 0)
            for c in range(C):
                sp.dma_start(wkv_s[:, c], wkv[:, c]).then_inc(S["l_wkv"], 16)
            for i in range(1, 4):
                load_xt(i, i)
            for w, src in (("q", qs), ("k", ks)):
                sp.dma_start(nscale[w][:], src.partition_broadcast(128)).then_inc(S["l_scale"], 16)
            sp.dma_start(wt_s, wt).then_inc(S["l_up"], 16)
            sp.dma_start(a2_s[:], a2t).then_inc(S["l_up"], 16)
            sp.dma_start(wpt_s, wpt).then_inc(S["l_up"], 16)
            sp.dma_start(b2_s[:], b2t).then_inc(S["l_up"], 16)

            def store_kv(n, i):
                sp.wait_ge(S["ka_rot"], n + 1)
                sp.wait_ge(S["ka_v"], n + 1)
                sp.dma_start(newkv_t[n], kvo[i][:]).then_inc(kv_stored[i], 16)

            sp.dma_start(wq_s[:], wq).then_inc(S["l_wq"], 16)
            sp.dma_start(wo_s[:], wo).then_inc(S["l_wo"], 16)
            sp.dma_start(wb_s[:], wb).then_inc(S["l_wb"], 16)
            sp.dma_start(w3_s[:], w3).then_inc(S["l_w3"], 16)
            sp.dma_start(a3_s[:], a3t).then_inc(S["l_w3"], 16)
            sp.dma_start(b3_s[:], b3t).then_inc(S["l_w3"], 16)

            with sp.Fori(0, TILES // 4 - 1) as j:
                for i in range(4):
                    sp.wait_ge(S["ka_mm"], j * 4 + (i + 1))
                    load_xt(j * 4 + (i + 4), i)
                    store_kv(j * 4 + i, i % 2)
            for n in range(TILES - 4, TILES):
                store_kv(n, n % 2)

            def load_xq(n, before):
                after(sp, S["q_mm"], before)
                sp.dma_start(xt_s[0][:], xt[n]).then_inc(S["l_xq"], 16)

            def tile(t, first, last):
                if not last:
                    load_xq(t.n(1, 1), t.n(1, 1))
                after(sp, S["x1_ready"], t.n(1, 0))
                sp.dma_start(xtok_s[:], xtok[t.n(1, 0)]).then_inc(S["l_xtok"], 16)
                sp.dma_start(subj_s[:], subj[t.n(1, 0)]).then_inc(S["l_subj"], 16)
                after(sp, S["w1i_ready"], t.n(1, 0))
                wait_alone(sp, (S["l_subj"], t.n(16, 16)))
                for u in range(2):
                    s = sp.value_load(subj_s[0:1, u:u + 1], min_val=0, max_val=7)
                    sp.dma_start(w1raw[64 * u:64 * u + 64, 64 * u:64 * u + 64], w1[s]).then_inc(S["l_w1"], 16)
                if not first:
                    sp.wait_ge(S["xo_ready"], t.n(1, 0))
                    sp.dma_start(out[t.n(1, -1)], xo[:]).then_inc(S["stored"], 16)

            sp.wait_ge(S["ka_mm"], TILES)
            load_xq(0, 0)
            sp.wait_ge(S["zeroed"], 1)
            tile(Tile(0, 0), True, False)
            with sp.Fori(0, TILES // 2 - 1) as j:
                for c in (1, 2):
                    tile(Tile(j, c), False, False)
            tile(Tile(TILES // 2 - 1, 1), False, True)
            sp.wait_ge(S["xo_ready"], TILES)
            sp.dma_start(out[TILES - 1], xo[:]).then_inc(S["stored"], 16)
            sp.wait_ge(S["stored"], 16 * (TILES + 1))

        @block.gpsimd
        def _(pool):
            nc.gpsimd.dma_start(tab_i[:], table).then_inc(S["l_table"], 16)
            nc.gpsimd.dma_start(kvc[:, 0:1], kvl.rearrange("(b a) -> b a", a=1)).then_inc(S["l_table"], 16)
            nc.gpsimd.memset(half[:], -0.5)
            nc.gpsimd.memset(qz[:], 0.0)
            nc.gpsimd.memset(up2[:], 0.0)
            nc.gpsimd.memset(z2m[:], 0.0)
            nc.gpsimd.memset(w1raw[:], 0.0).then_inc(S["zeroed"], 1)
            pool.wait_ge(S["zeroed"], 1)

            def rstd(w, h, ready, done, value):
                pool.wait_ge(S[ready], value)
                nc.gpsimd.tensor_tensor(nr[w]["rstd"][:], nr[w]["ms"][:], half[:, 0:h], ALU.pow).then_inc(S[done], 1)

            with pool.Fori(0, TILES) as i:
                rstd("k", 4, "ka_ms", "ka_rstd", i + 1)

            for name, w in (("l_wb", wb_s), ("l_w3", w3_s)):
                pool.wait_ge(S[name], 16 if name == "l_wb" else 48)
                for c in range(C):
                    d = w[:, c, 128 * c:128 * c + 128]
                    last = nc.gpsimd.tensor_tensor(d, d, ident, ALU.add)
            last.then_inc(S["w_ident"], 1)

            def copy_index(t, u, k):
                i = (t.part(u) + k) % 2
                n = t.b(u, 1, k)
                src = idx_all[:, n:n + 1, :] if isinstance(n, int) else idx_all[:, bass.ds(n, 1), :]
                nc.gpsimd.tensor_copy(idx_b[i][:], src.rearrange("p a k -> p (a k)")).then_inc(S["idx_copied"], 1)

            def gather(t, u, k, new):
                r, done = t.ring(u + k)
                i = (t.part(u) + k) % 2
                for c in range(CH):
                    nc.gpsimd.indirect_dma_start(
                        kv_s[r][:, c, :], None, newkv if new else kvrows,
                        bass.IndirectOffsetOnAxis(ap=idx_b[i][:, new * CH + c:new * CH + c + 1], axis=0),
                        bounds_check=(NB * NT if new else NPOOL * BLOCK) - 1, oob_is_err=False,
                    ).then_inc((kv_new if new else kv_old)[r], 16)

            def lay_over(t, u, k):
                r, done = t.ring(u + k)
                wait_alone(pool, (kv_old[r], done))
                gather(t, u, k, 1)

            def norm(t, u, k):
                i = (t.part(u) + k) % 2
                for g in range(G):
                    wait_alone(pool, (S["rinv_ready"], t.b(u, 2, 2 * k + g // 2 + 1)))
                    nc.gpsimd.tensor_scalar(prob[i][:, g, :], prob[i][:, g, :], rinv[i][:, g:g + 1], 1.0,
                                            ALU.mult, ALU.mult).then_inc(S["prob_ready"], 1)

            def w1_ident(t):
                pool.wait_ge(S["l_w1"], t.n(32, 32))
                after(pool, S["l1_mm"], t.n(1, 0))
                nc.gpsimd.tensor_tensor(w1i[:], w1raw[:], ident, ALU.add).then_inc(S["w1i_ready"], 1)

            def slot(t, u, b_left):
                if u == 1 and b_left > 0:
                    rstd("q", 8, "q_ms", "q_rstd", t.n(1, 2))
                if b_left >= 3:
                    r, done = t.ring(u + 1)
                    pool.wait_ge(kv_new[r], done)
                    copy_index(t, u, 3)
                    wait_alone(pool, (S["idx_copied"], t.b(u, 1, 4)), (S["pv_mm"], t.b(u, 2, 0)))
                    gather(t, u, 3, 0)
                if b_left >= 2:
                    lay_over(t, u, 2)
                if u == 1:
                    w1_ident(t)
                if b_left >= 1:
                    norm(t, u, 1)

            t0 = Tile(0, 0)
            pool.wait_ge(S["idx_ready"], 1)
            rstd("q", 8, "q_ms", "q_rstd", 1)
            for k in range(2):
                copy_index(t0, 0, k)
                pool.wait_ge(S["idx_copied"], k + 1)
                gather(t0, 0, k, 0)
            for i in range(2):
                pool.wait_ge(kv_stored[i], 16 * TILES // 2)
            for k in range(2):
                lay_over(t0, 0, k)
            r, done = t0.ring(0)
            pool.wait_ge(kv_new[r], done)
            copy_index(t0, 0, 2)
            pool.wait_ge(S["idx_copied"], 3)
            gather(t0, 0, 2, 0)
            norm(t0, 0, 0)
            slot(t0, 0, NB - 1)
            slot(t0, 1, NB - 2)
            with pool.Fori(0, TILES // 2 - 2) as j:
                for c in (1, 2):
                    for u in range(2):
                        slot(Tile(j, c), u, 3)
            for c in (1, 2, 3):
                for u in range(2):
                    slot(Tile(TILES // 2 - 2, c), u, 2 * (3 - c) + 1 - u)

        @block.scalar
        def _(act):
            act.dma_start(kvb[:], kvl.partition_broadcast(128)).then_inc(S["l_kv"], 16)
            act.dma_start(cst[:], const).then_inc(S["l_const"], 16)
            for d, s in ((scl2[0:64], s2), (scl3[:], s3), (idx2[:], ad2.partition_broadcast(128)),
                         (idx3[:], ad3.partition_broadcast(128))):
                act.dma_start(d, s).then_inc(S["l_ad"], 16)
            act.wait_ge(S["tab_ready"], 1)
            nc.scalar.activation(sinx[:], rest[:], ACT.Sin)
            nc.scalar.activation(cosx[:], turns[:], ACT.Sin).then_inc(S["sin_done"], 1)

            def key_tile(n, i, free):
                act.wait_ge(S["ka_mm"], n + 1)
                after(act, S["ka_ss"], n)
                nc.scalar.activation(nr["k"]["sq"][:], gb[i][:, 0:256].rearrange("p (g d) -> p g d", g=G),
                                     ACT.Square).then_inc(S["ka_sq"], 1)
                after(act, kv_stored[i], free)
                nc.scalar.activation(kvo[i][:, 256:512], gb[i][:, 256:512], ACT.Copy).then_inc(S["ka_v"], 1)

            for n in range(2):
                key_tile(n, n % 2, 0)
            with act.Fori(1, TILES // 2) as j:
                for i in range(2):
                    key_tile(j * 2 + i, i, j * 16)
            act.wait_ge(S["down_mm"], 1)
            nc.scalar.activation(down2[:], ob[0][:, 0:C * 64].rearrange("p (c r) -> p c r", c=C), ACT.Copy).then_inc(S["down_ev"], 1)
            act.wait_ge(S["zeroed"], 1)
            act.wait_ge(S["up_mm"], 1)
            nc.scalar.activation(up2[0:64, :], ob[1][0:64, :], ACT.Copy).then_inc(S["up_ev"], 1)

            def square(n):
                act.wait_ge(S["q_mm"], n)
                nc.scalar.activation(nr["q"]["sq"][:], gb[0][:].rearrange("p (h d) -> p h d", h=8),
                                     ACT.Square).then_inc(S["q_sq"], 1)

            def queries(n, used):
                act.wait_ge(S["qt_mm"], n)
                after(act, S["s_mm"], used)
                for h in range(2):
                    nc.scalar.activation(qz[64 * h:64 * h + 64, h], gb[1][64 * h:64 * h + 64, :],
                                         ACT.Copy).then_inc(S["qz_ready"], 1)

            def exps(t, u, k, g):
                i = (t.part(u) + k) % 2
                act.wait_ge(S["negs_ready"], t.b(u, 4, 4 * k + g + 1))
                after(act, S["pt_mm"], t.b(u, 4, 4 * (k - 2) + g + 1))
                nc.scalar.activation(prob[i][:, g, :], neg_s[:, g, :], ACT.Exp, bias=negmax[:, g:g + 1], scale=-1.0,
                                     accum_out=psum_p[i][:, g:g + 1]).then_inc(S["exp_done"], 1)

            def probs_t(t, u, g):
                act.wait_ge(S["pt_mm"], t.b(u, 4, g + 1))
                after(act, S["pv_mm"], t.b(u, 2, g // 2 - 1))
                nc.scalar.activation(pt_s[g][:], tb[g % 2][0:KP, 0:CH * 128].rearrange("p (c q) -> p c q", c=CH),
                                     ACT.Copy).then_inc(S["pt_ev"], 1)

            def attn_out(t, u):
                act.wait_ge(S["pv_mm"], t.b(u, 2, 2))
                after(act, S["wo_mm"], t.n(1, 0))
                nc.scalar.activation(ot_s[:, :, 64 * u:64 * u + 64],
                                     ob[u][:, 0:256].rearrange("p (k t) -> p k t", k=4), ACT.Copy).then_inc(S["ot_ev"], 1)

            def evac(src, dst, ready, value, done):
                act.wait_ge(S[ready], value)
                nc.scalar.activation(dst, src, ACT.Copy).then_inc(S[done], 1)

            def layer1(t):
                evac(gb[1][:].rearrange("p (c t) -> p c t", c=C), x2t[:], "l1_mm", t.n(1, 0), "x2_ready")

            def layer2(t):
                evac(gb[1][:].rearrange("p (c t) -> p c t", c=C), x3t[:], "x3_mm", t.n(1, 0), "x3_ready")

            def layer3(t):
                act.wait_ge(S["out_mm"], t.n(1, 0))
                act.wait_ge(S["stored"], t.n(16, 0))
                nc.scalar.activation(xo[:], gb[0][:], ACT.Copy).then_inc(S["xo_ready"], 1)

            def tile(t, first, last):
                exps(t, 0, 1, 0)
                exps(t, 0, 1, 1)
                probs_t(t, 0, 0)
                probs_t(t, 0, 1)
                exps(t, 0, 1, 2)
                if not first:
                    layer1(t)
                exps(t, 0, 1, 3)
                probs_t(t, 0, 2)
                probs_t(t, 0, 3)
                attn_out(t, 0)
                if not first:
                    layer2(t)
                if not last:
                    square(t.n(1, 2))
                if not first:
                    layer3(t)
                if not last:
                    queries(t.n(1, 2), t.b(1, 4, 4))
                for g in range(4):
                    probs_t(t, 1, g)
                if not last:
                    for g in range(3):
                        exps(t, 1, 1, g)
                attn_out(t, 1)
                if not last:
                    exps(t, 1, 1, 3)

            act.sem_inc(S["stored"], 16)
            square(1)
            queries(1, 0)
            for g in range(G):
                exps(Tile(0, 0), 0, 0, g)
            tile(Tile(0, 0), True, False)
            with act.Fori(0, TILES // 2 - 1) as j:
                for c in (1, 2):
                    tile(Tile(j, c), False, False)
            tile(Tile(TILES // 2 - 1, 1), False, True)
            end = Tile(TILES // 2, 0)
            layer1(end)
            layer2(end)
            layer3(end)

        @block.vector
        def _(dve):
            n_set = [0]

            def link(ins):
                n_set[0] += 1
                ins.then_inc(S["set_dve"], 1)
                dve.wait_ge(S["set_dve"], n_set[0])

            V = nc.vector
            dve.wait_ge(S["l_kv"], 16)
            V.tensor_scalar(kvi[:], kvb[:], 4, None, ALU.arith_shift_right)
            V.tensor_copy(pos[0:64, :], kvb[0:64].rearrange("p (n u) -> p n u", u=2)[:, :, 0])
            link(V.tensor_copy(pos[64:128, :], kvb[64:128].rearrange("p (n u) -> p n u", u=2)[:, :, 1]))
            link(V.tensor_copy(k0f[:], kvi[:]))
            V.tensor_copy(r0f[:], kvb[:])
            dve.wait_ge(S["l_const"], 16)
            link(V.tensor_scalar(pos[:], pos[:], con("tpos"), None, ALU.add))
            V.scalar_tensor_tensor(r0f[:], k0f[:], -16.0, r0f[:], ALU.mult, ALU.add)
            inv = con("inv").unsqueeze(1).to_broadcast([128, TILES, 32])
            link(V.tensor_tensor(ang[:], pos[:].unsqueeze(2).to_broadcast([128, TILES, 32]), inv, ALU.mult))
            MAGIC = 1.5 * 2.0 ** 23
            link(V.tensor_scalar(turns[:], ang[:], float(1.0 / (2.0 * np.pi)), MAGIC, ALU.mult, ALU.add))
            link(V.tensor_scalar(turns[:], turns[:], -MAGIC, None, ALU.add))
            c1 = 6.28125
            c2 = float(np.float32(np.round((2 * np.pi - c1) * 2.0 ** 22) / 2.0 ** 22))
            c3 = float(np.float32(2 * np.pi - c1 - c2))
            link(V.scalar_tensor_tensor(rest[:], turns[:], -c1, ang[:], ALU.mult, ALU.add))
            link(V.scalar_tensor_tensor(rest[:], turns[:], -c2, rest[:], ALU.mult, ALU.add))
            link(V.scalar_tensor_tensor(rest[:], turns[:], -c3, rest[:], ALU.mult, ALU.add))
            link(V.tensor_scalar(rest[:], rest[:], 3.1415925, -3.1415925, ALU.min, ALU.max))
            link(V.scalar_tensor_tensor(turns[:], rest[:], -1.0, rest[:], ALU.mult, ALU.max))
            V.tensor_scalar(turns[:], turns[:], -1.0, float(np.pi / 2), ALU.mult, ALU.add).then_inc(S["tab_ready"], 1)
            V.tensor_scalar(band[:], r0f[:], 2.0, WINDOW + 1.0, ALU.mult, ALU.add)
            V.tensor_scalar(start[:], k0f[:], -160000.0, 2555000.0, ALU.mult, ALU.add)
            link(V.tensor_scalar(limit[:], r0f[:], -1.0, -WINDOW - 0.5, ALU.mult, ALU.add))
            V.scalar_tensor_tensor(limit[:], r0f[:], 0.5, limit[:], ALU.add, ALU.mult)
            dve.wait_ge(S["l_ad"], 64)
            V.tensor_scalar(pick2[0:64], idx2[0:64], con("e2", 64), scl2[0:64], ALU.is_equal, ALU.mult)
            V.tensor_scalar(pick3[:], idx3[:], con("e3"), scl3[:], ALU.is_equal, ALU.mult)
            dve.wait_ge(S["l_scale"], 32)
            V.tensor_scalar(nscale["q"][:], nscale["q"][:], 1.0, None, ALU.add)
            link(V.tensor_scalar(nscale["k"][:], nscale["k"][:], 1.0, None, ALU.add))
            dve.wait_ge(S["sin_done"], 1)
            for w in ("k", "q"):
                lo, hi = (nscale[w][:, 32 * a:32 * a + 32].unsqueeze(1).to_broadcast([128, TILES, 32]) for a in (0, 1))
                V.tensor_tensor(costab[w][:, :, 0:32], cosx[:], lo, ALU.mult)
                V.tensor_tensor(costab[w][:, :, 32:64], cosx[:], hi, ALU.mult)
                V.tensor_tensor(sintab[w][:, :, 32:64], sinx[:], lo, ALU.mult)
                V.tensor_tensor(sintab[w][:, :, 0:32], sinx[:], hi, ALU.mult)
                last = V.tensor_copy(nr[w]["ss"][:, 0:1], nscale[w][:, 0:1])
                link(last)
                link(V.tensor_scalar(sintab[w][:, :, 0:32], sintab[w][:, :, 0:32], -1.0, None, ALU.mult))

            def norm_rotate(w, h, src, dst, tab, names, value, gate=None, between=None):
                sq_d, ss_d, ms_d, rstd_d, n_d, t2_d, rot_d = names
                k = nr[w]
                dve.wait_ge(S[sq_d], value)
                V.reduce_sum(k["ss"][:], k["sq"][:], AX).then_inc(S[ss_d], 1)
                dve.wait_ge(S[ss_d], value)
                V.tensor_scalar(k["ms"][:], k["ss"][:], 1.0 / HD, 1e-6, ALU.mult, ALU.add).then_inc(S[ms_d], 1)
                if between:
                    between()
                if w == "k":
                    dve.wait_ge(S["ka_v"], value)
                dve.wait_ge(S[rstd_d], value)
                V.tensor_tensor(k["n"][:], src, k["rstd"][:].unsqueeze(2).to_broadcast([128, h, 64]),
                                ALU.mult).then_inc(S[n_d], 1)
                cos, sin = (x[w][:, tab:tab + 1, :] if isinstance(tab, int) else x[w][:, bass.ds(tab, 1), :] for x in (costab, sintab))
                dve.wait_ge(S[n_d], value)
                V.tensor_tensor(k["t1"][:], k["n"][:], cos.to_broadcast([128, h, 64]), ALU.mult)
                V.tensor_tensor(k["t2"][:, :, 0:32], k["n"][:, :, 32:64], sin[:, :, 0:32].to_broadcast([128, h, 32]), ALU.mult)
                V.tensor_tensor(k["t2"][:, :, 32:64], k["n"][:, :, 0:32], sin[:, :, 32:64].to_broadcast([128, h, 32]),
                                ALU.mult).then_inc(S[t2_d], 1)
                if gate:
                    gate()
                dve.wait_ge(S[t2_d], value)
                V.tensor_tensor(dst, k["t1"][:], k["t2"][:], ALU.add).then_inc(S[rot_d], 1)

            KN = ("ka_sq", "ka_ss", "ka_ms", "ka_rstd", "ka_n", "ka_t2", "ka_rot")
            QN = ("q_sq", "q_ss", "q_ms", "q_rstd", "q_n", "q_t2", "q_rot")

            def key_tile(n, i, free):
                norm_rotate("k", 4, gb[i][:, 0:256].rearrange("p (g d) -> p g d", g=G),
                            kvo[i][:, 0:256].rearrange("p (g d) -> p g d", g=G), n, KN, n + 1,
                            gate=lambda: after(dve, kv_stored[i], free))

            for n in range(2):
                key_tile(n, n, 0)
            with dve.Fori(1, HALF_A // 2) as j:
                for i in range(2):
                    key_tile(j * 2 + i, i, j * 16)

            dve.wait_ge(S["l_table"], 32)
            V.tensor_copy(tab_f[:], tab_i[:])
            link(V.tensor_scalar(kvc[:, 1:2], kvc[:, 0:1], 4, None, ALU.arith_shift_right))
            V.tensor_copy(kvcf[:, 1:2], kvc[:, 0:1])
            link(V.tensor_copy(kvcf[:, 0:1], kvc[:, 1:2]))
            V.scalar_tensor_tensor(kvcf[:, 1:2], kvcf[:, 0:1], -16.0, kvcf[:, 1:2], ALU.mult, ALU.add)
            link(V.tensor_scalar(want[:], con("win", NB), kvcf[:, 0:1], None, ALU.add))
            for s in range(WS):
                link(V.scalar_tensor_tensor(hit[:], con("slots", NB), want[:, s:s + 1], tab_f[:], ALU.is_equal, ALU.mult,
                                            accum_out=blk[:, s:s + 1]))
            V.tensor_tensor(blkd[:], blk[:].unsqueeze(2).to_broadcast([NB, WS, NB]),
                            con("ident", NB)[:, 0:NB].unsqueeze(1).to_broadcast([NB, WS, NB]), ALU.mult).then_inc(S["blkd_ready"], 1)
            link(V.tensor_scalar(wt_tok[:], con("toff", NB), kvcf[:, 1:2], None, ALU.subtract))
            V.tensor_scalar(code[:], wt_tok[:], con("code", NB), None, ALU.add)
            link(V.tensor_scalar(wt_ge[:], wt_tok[:], 0.0, None, ALU.is_ge))
            link(V.scalar_tensor_tensor(cover[:], wt_tok[:], float(NT), wt_ge[:], ALU.is_lt, ALU.mult))
            dve.wait_ge(S["blkrow_mm"], 1)
            HW = WS * NB // 2
            brow = blkrow[:].rearrange("p s b -> p (s b)")
            for i in range(2):
                last = V.tensor_copy(brow[:, HW * i:HW * i + HW], sbk[i][0:NB, 0:HW])
            link(last)
            for j in range(NW):
                last = V.tensor_scalar(same[:, j, :], brow, blk[:, WS - NW + j:WS - NW + j + 1], None, ALU.is_equal)
            last.then_inc(S["same_ready"], 1)
            dve.wait_ge(S["same_ready"], 1)
            V.tensor_tensor(later[:], same[:, :, (WS - NW) * NB:], con("order", NB).rearrange("p (j e) -> p j e", j=NW),
                            ALU.mult).then_inc(S["later_ready"], 1)
            link(V.tensor_scalar(rows[:, 0, :], brow[0:BLOCK], float(BLOCK), con("off", BLOCK), ALU.mult, ALU.add))
            dve.wait_ge(S["lose_mm"], 1)
            link(V.scalar_tensor_tensor(wins[:], tb[0][0:NB, 0:NW * BLOCK], 0.0, cover[:], ALU.is_equal, ALU.mult))
            V.tensor_tensor(wcode[:], wins[:], code[:], ALU.mult).then_inc(S["wcode_ready"], 1)
            dve.wait_ge(S["win_mm"], 1)
            for i in range(2):
                w = sbk[i][0:BLOCK, 0:HW]
                link(V.tensor_scalar(none[:, HW * i:HW * i + HW], w, 0.0, float(NONE), ALU.is_equal, ALU.mult))
                last = V.scalar_tensor_tensor(rows[:, 1, HW * i:HW * i + HW], w, -1.0, none[:, HW * i:HW * i + HW], ALU.add, ALU.add)
            last.then_inc(S["rows_ready"], 1)
            dve.wait_ge(S["idx_mm"], 1)
            V.tensor_copy(idx_all[:], tb[1][0:KP, 0:2 * CH * NB].rearrange("p (k b) -> p b k", b=NB)).then_inc(S["idx_ready"], 1)

            with dve.Fori(HALF_A // 2, TILES // 2) as j:
                for i in range(2):
                    key_tile(j * 2 + i, i, j * 16)

            dve.wait_ge(S["zeroed"], 1)

            def make_mask(t, u, k):
                m = mask[(t.part(u) + k) % 2]
                n = t.b(u, 1, k)
                col = (lambda a: a[:, n:n + 1]) if isinstance(n, int) else (lambda a: a[:, bass.ds(n, 1)])
                V.scalar_tensor_tensor(m[:], con("diff"), col(band), con("diff"), ALU.subtract, ALU.mult).then_inc(S["mask_band"], 1)
                dve.wait_ge(S["mask_band"], t.b(u, 1, k + 1))
                V.scalar_tensor_tensor(m[:], con("negc"), col(start), m[:], ALU.add, ALU.max).then_inc(S["mask_start"], 1)
                dve.wait_ge(S["mask_start"], t.b(u, 1, k + 1))
                V.tensor_scalar(m[:], m[:], col(limit), -NEG, ALU.is_gt, ALU.mult).then_inc(S["mask_ready"], 1)

            def keys_t(t, u, k):
                for p in range(2):
                    dve.wait_ge(S["kt_mm"], t.b(u, 2, 2 * k + p + 1))
                    after(dve, S["s_mm"], t.b(u, 4, 4 * k - 2 + 2 * p))
                    V.tensor_copy(kt_s[:, p, :], tb[p][:, 0:WK]).then_inc(S["kt_ev"], 1)

            def scores(t, u, k):
                dve.wait_ge(S["mask_ready"], t.b(u, 1, k + 1))
                for g in range(G):
                    wait_alone(dve, (S["s_mm"], t.b(u, 4, 4 * k + g + 1)),
                               (S["exp_done"], t.b(u, 4, 4 * (k - 1) + g + 1)))
                    V.tensor_tensor_reduce(out=neg_s[:, g, :], in0=sbk[g % 2][:, 0:WK], in1=mask[(t.part(u) + k) % 2][:],
                                           scale=-1.0 / 16, scalar=3.0e38, op0=ALU.add, op1=ALU.min,
                                           accum_out=negmax[:, g:g + 1]).then_inc(S["negs_ready"], 1)

            def inverse(t, u, k):
                i = (t.part(u) + k) % 2
                for p in range(2):
                    dve.wait_ge(S["exp_done"], t.b(u, 4, 4 * k + 2 * p + 2))
                    V.reciprocal(rinv[i][:, 2 * p:2 * p + 2], psum_p[i][:, 2 * p:2 * p + 2]).then_inc(S["rinv_ready"], 1)

            def query_tile(t, plus, between):
                norm_rotate("q", 8, gb[0][:].rearrange("p (h d) -> p h d", h=8), qrot[:].rearrange("p (h d) -> p h d", h=8),
                            t.n(1, plus), QN, t.n(1, plus + 1), between=between,
                            gate=lambda: after(dve, S["qt_mm"], t.n(1, plus)))

            def attn_residual(t):
                dve.wait_ge(S["wo_mm"], t.n(1, 0))
                dve.wait_ge(S["l_xtok"], t.n(16, 0))
                V.tensor_tensor(x1[:], gb[0][:], xtok_s[:], ALU.add).then_inc(S["x1_ready"], 1)

            def pick(t, z, ready, picks, rows_, bank, done):
                dve.wait_ge(S[ready], t.n(1, 0))
                n = t.n(2, -2)
                p = picks[0:rows_, n:n + 2] if isinstance(n, int) else picks[0:rows_, bass.ds(n, 2)]
                V.tensor_tensor(z[0:rows_, :].rearrange("p (u t) -> p u t", u=2),
                                gb[bank][0:rows_, 0:128].rearrange("p (u t) -> p u t", u=2),
                                p.unsqueeze(2).to_broadcast([rows_, 2, 64]), ALU.mult).then_inc(S[done], 1)

            def tile(t, first, last):
                keys_t(t, 0, 1)
                make_mask(t, 0, 1)
                if not first:
                    attn_residual(t)
                scores(t, 0, 1)
                inverse(t, 0, 1)
                if not first:
                    pick(t, z2m, "z2_mm", pick2, 64, 0, "z2_ready")
                if not last:
                    def between():
                        keys_t(t, 1, 1)
                        if not first:
                            pick(t, z3m, "z3_mm", pick3, 128, 1, "z3_ready")
                        make_mask(t, 1, 1)
                    query_tile(t, 1, between)
                    scores(t, 1, 1)
                    inverse(t, 1, 1)
                else:
                    pick(t, z3m, "z3_mm", pick3, 128, 1, "z3_ready")

            t0 = Tile(0, 0)

            def first_keys():
                make_mask(t0, 0, 0)
            query_tile(t0, 0, first_keys)
            keys_t(t0, 0, 0)
            scores(t0, 0, 0)
            inverse(t0, 0, 0)
            tile(t0, True, False)
            with dve.Fori(0, TILES // 2 - 1) as j:
                for c in (1, 2):
                    tile(Tile(j, c), False, False)
            tile(Tile(TILES // 2 - 1, 1), False, True)
            end = Tile(TILES // 2, 0)
            attn_residual(end)
            pick(end, z2m, "z2_mm", pick2, 64, 0, "z2_ready")
            pick(end, z3m, "z3_mm", pick3, 128, 1, "z3_ready")

        @block.tensor
        def _(pe):
            mm = nc.tensor.matmul

            def dense(bank, lhs, rhs, more=None):
                for c in range(C):
                    last = mm(bank, lhs(c), rhs(c), start=(c == 0), stop=(c == C - 1 and more is None))
                return last

            def key_tile(n, r, rounds, free):
                i = r % 2
                pe.wait_ge(l_xt[r], rounds)
                if not isinstance(free, int) or free > 0:
                    pe.wait_ge(S["ka_n"], free)
                    pe.wait_ge(S["ka_v"], free)
                dense(gb[i][:], lambda c: xt_s[r][:, c, :], lambda c: wkv_s[:, c, :]).then_inc(S["ka_mm"], 1)

            pe.wait_ge(S["l_wkv"], 16 * C)
            for n in range(4):
                key_tile(n, n, 16, n - 1)
            with pe.Fori(1, HALF_A // 4) as j:
                for r in range(4):
                    key_tile(None, r, j * 16 + 16, j * 4 + (r - 1))

            pe.wait_ge(S["l_up"], 64)
            for c in range(C):
                for k in range(C):
                    last = mm(ob[0][:, 64 * c:64 * c + 64], wt_s[:, k, 128 * c:128 * c + 128], a2_s[:, k, :],
                              start=(k == 0), stop=(k == C - 1))
            last.then_inc(S["down_mm"], 1)
            dense(ob[1][0:64, :], lambda c: b2_s[:, c, :], lambda c: wpt_s[:, c, :]).then_inc(S["up_mm"], 1)

            HW = WS * NB // 2
            pe.wait_ge(S["blkd_ready"], 1)
            bd = blkd[:].rearrange("p s b -> p (s b)")
            for i in range(2):
                last = mm(sbk[i][0:NB, 0:HW], con("ones", NB), bd[:, HW * i:HW * i + HW], start=True, stop=True)
            last.then_inc(S["blkrow_mm"], 1)
            pe.wait_ge(S["later_ready"], 1)
            for j in range(NW):
                for k in range(NW):
                    last = mm(tb[0][0:NB, BLOCK * j:BLOCK * j + BLOCK], later[:, k, NB * j:NB * j + NB],
                              cover[:, BLOCK * k:BLOCK * k + BLOCK], start=(k == 0), stop=(k == NW - 1))
            last.then_inc(S["lose_mm"], 1)
            pe.wait_ge(S["wcode_ready"], 1)
            for i in range(2):
                for j in range(NW):
                    last = mm(sbk[i][0:BLOCK, 0:HW], wcode[:, BLOCK * j:BLOCK * j + BLOCK], same[:, j, HW * i:HW * i + HW],
                              start=(j == 0), stop=(j == NW - 1))
            last.then_inc(S["win_mm"], 1)
            pe.wait_ge(S["rows_ready"], 1)
            spread = con("spread", BLOCK).rearrange("p (s q) -> p s q", s=SP_)
            for k in range(2):
                src = rows[:, k, :].rearrange("p (c s b) -> p s c b", c=CH, s=SP_)
                for s in range(SP_):
                    last = mm(tb[1][0:KP, CH * NB * k:CH * NB * (k + 1)].rearrange("p (c b) -> p c b", c=CH),
                              spread[:, s, :], src[:, s], start=(s == 0), stop=(s == SP_ - 1))
            last.then_inc(S["idx_mm"], 1)

            with pe.Fori(HALF_A // 4, TILES // 4) as j:
                for r in range(4):
                    key_tile(None, r, j * 16 + 16, j * 4 + (r - 1))

            def queries(loads, bank_free):
                pe.wait_ge(S["l_xq"], loads)
                bank_free()
                dense(gb[0][:], lambda c: xt_s[0][:, c, :], lambda c: wq_s[:, c, :]).then_inc(S["q_mm"], 1)

            def queries_t(n):
                pe.wait_ge(S["q_rot"], n)
                o = gb[1][:].rearrange("p (a v q t) -> p a q v t", a=2, v=2, q=2)
                for k in range(4):
                    last = nc.tensor.transpose(o[:, k // 2, k % 2], qrot[:, 128 * k:128 * k + 128], ident)
                last.then_inc(S["qt_mm"], 1)

            def keys_t(t, u, k):
                r, done = t.ring(u + k)
                pe.wait_ge(kv_new[r], done)
                for p in range(2):
                    after(pe, S["pt_ev"], t.b(u, 4, 4 * (k - 2) + 3 + p))
                    for c in range(CH):
                        last = nc.tensor.transpose(tb[p][:, KP * c:KP * c + KP], kv_s[r][:, c, 128 * p:128 * p + 128],
                                                   ident[0:KP, 0:KP])
                    last.then_inc(S["kt_mm"], 1)

            def scores(t, u, k):
                if (t.part(u) + k) % 2 == 0:
                    pe.wait_ge(S["qz_ready"], t.n(2, 2 * ((u + k) // 2) + 2))
                for g in range(G):
                    p, h = g // 2, g % 2
                    pe.wait_ge(S["kt_ev"], t.b(u, 2, 2 * k + p + 1))
                    after(pe, S["negs_ready"], t.b(u, 4, 4 * k + g - 1))
                    v = (u + k) % 2
                    mm(sbk[g % 2][:, 0:WK], qz[:, h, 256 * p + 128 * v:256 * p + 128 * v + 128], kt_s[:, p, :],
                       start=True, stop=True).then_inc(S["s_mm"], 1)

            def probs_t(t, u, g, last_batch):
                i = t.part(u) % 2
                if g >= 2:
                    pe.wait_ge(S["pt_ev"], t.b(u, 4, g - 1))
                elif last_batch:
                    pe.wait_ge(S["pt_ev"], t.b(u, 4, g - 1))
                else:
                    pe.wait_ge(S["kt_ev"], t.b(u, 2, 2 + g + 1))
                pe.wait_ge(S["prob_ready"], t.b(u, 4, g + 1))
                for c in range(CH):
                    last = nc.tensor.transpose(tb[g % 2][0:KP, 128 * c:128 * c + 128], prob[i][:, g, KP * c:KP * c + KP], ident)
                last.then_inc(S["pt_mm"], 1)

            def values(t, u, p):
                r, _ = t.ring(u)
                pe.wait_ge(S["pt_ev"], t.b(u, 4, 2 * p + 2))
                after(pe, S["ot_ev"], t.b(u, 1, -1))
                for c in range(CH):
                    for h in range(2):
                        g = 2 * p + h
                        last = mm(ob[u][64 * h:64 * h + 64, 128 * p:128 * p + 128], kv_s[r][:, c, 256 + 64 * g:320 + 64 * g],
                                  pt_s[g][:, c, :], start=(c == 0), stop=(c == CH - 1))
                last.then_inc(S["pv_mm"], 1)

            def project(t):
                pe.wait_ge(S["ot_ev"], t.b(0, 1, 0))
                dense(gb[0][:], lambda c: ot_s[:, c, :], lambda c: wo_s[:, c, :]).then_inc(S["wo_mm"], 1)

            def layer1(t, queries_in_bank):
                pe.wait_ge(S["x1_ready"], t.n(1, 0))
                pe.wait_ge(S["w1i_ready"], t.n(1, 0))
                if queries_in_bank:
                    pe.wait_ge(S["qz_ready"], t.n(2, 2))
                for c in range(C):
                    last = mm(gb[1][:, 128 * c:128 * c + 128], x1[:, 128 * c:128 * c + 128], w1i[:], start=True, stop=True)
                last.then_inc(S["l1_mm"], 1)

            def ranks2(t):
                pe.wait_ge(S["x2_ready"], t.n(1, 0))
                dense(gb[0][0:64, 0:128], lambda c: down2[:, c, :], lambda c: x2t[:, c, :]).then_inc(S["z2_mm"], 1)

            def layer2(t):
                for k in range(C):
                    o = gb[1][:, 128 * k:128 * k + 128]
                    dense(o, lambda c: wb_s[:, c, 128 * k:128 * k + 128], lambda c: x2t[:, c, :], more=True)
                    if k == 0:
                        pe.wait_ge(S["z2_ready"], t.n(1, 0))
                    last = mm(o, up2[:, 128 * k:128 * k + 128], z2m[:], start=False, stop=True)
                last.then_inc(S["x3_mm"], 1)

            def ranks3(t):
                pe.wait_ge(S["x3_ready"], t.n(1, 0))
                dense(gb[1][:, 0:128], lambda c: a3_s[:, c, :], lambda c: x3t[:, c, :]).then_inc(S["z3_mm"], 1)

            def layer3(t, queries_in_bank):
                if queries_in_bank:
                    pe.wait_ge(S["q_n"], t.n(1, 2))
                dense(gb[0][:], lambda c: x3t[:, c, :], lambda c: w3_s[:, c, :], more=True)
                pe.wait_ge(S["z3_ready"], t.n(1, 0))
                mm(gb[0][:], z3m[:], b3_s[:], start=False, stop=True).then_inc(S["out_mm"], 1)

            def tile(t, first, last):
                keys_t(t, 0, 1)
                if not first:
                    project(t)
                scores(t, 0, 1)
                probs_t(t, 0, 0, False)
                probs_t(t, 0, 1, False)
                if not first:
                    layer1(t, True)
                values(t, 0, 0)
                probs_t(t, 0, 2, False)
                probs_t(t, 0, 3, False)
                if not first:
                    ranks2(t)
                values(t, 0, 1)
                if not first:
                    layer2(t)
                if not last:
                    queries(t.n(16, 32), (lambda: pe.wait_ge(S["q_n"], 1)) if first else (lambda: None))
                    keys_t(t, 1, 1)
                if not first:
                    ranks3(t)
                    layer3(t, not last)
                if not last:
                    queries_t(t.n(1, 2))
                probs_t(t, 1, 0, last)
                probs_t(t, 1, 1, last)
                values(t, 1, 0)
                probs_t(t, 1, 2, last)
                probs_t(t, 1, 3, last)
                if not last:
                    scores(t, 1, 1)
                values(t, 1, 1)

            pe.wait_ge(S["l_wq"], 16)

            def keys_out():
                pe.wait_ge(S["ka_n"], TILES)
                pe.wait_ge(S["ka_v"], TILES)
            queries(16, keys_out)
            pe.wait_ge(S["idx_ready"], 1)
            pe.wait_ge(S["down_ev"], 1)
            pe.wait_ge(S["up_ev"], 1)
            pe.wait_ge(S["w_ident"], 1)
            pe.wait_ge(S["l_wo"], 16)
            queries_t(1)
            keys_t(Tile(0, 0), 0, 0)
            scores(Tile(0, 0), 0, 0)
            tile(Tile(0, 0), True, False)
            with pe.Fori(0, TILES // 2 - 1) as j:
                for c in (1, 2):
                    tile(Tile(j, c), False, False)
            tile(Tile(TILES // 2 - 1, 1), False, True)
            end = Tile(TILES // 2, 0)
            project(end)
            layer1(end, False)
            ranks2(end)
            layer2(end)
            ranks3(end)
            layer3(end, False)


def kernel(x, itok_Bx257_0_4111, itok_B_37_3939, itok_B_0_7, itok_B_0_3, itok_B_0_6,
           L0_cond_Wq, L0_cond_Wk, L0_cond_Wv, L0_cond_Wo, L0_cond_q_norm_scale, L0_cond_k_norm_scale,
           L0_cond_k_blocks, L0_cond_v_blocks, L1_cond_weights, L2_cond_W_base, L2_cond_Wt, L2_cond_A,
           L2_cond_B_w, L2_cond_Wp, L2_cond_scaling, L3_cond_W, L3_cond_A, L3_cond_Bm, L3_cond_scalings):
    import concourse.bacc as bacc
    from concourse.bass_utils import run_bass_kernel_spmd

    def chunks(a):
        a = np.asarray(a)
        return np.ascontiguousarray(a.reshape(-1, 128, a.shape[1]).transpose(1, 0, 2))

    x = np.asarray(x)
    xf = x.reshape(TILES, 128, D)
    wq = np.asarray(L0_cond_Wq).T.reshape(D, 2, 2, 2, HD)
    wo = np.asarray(L0_cond_Wo).T.reshape(2, 2, 2, HD, D)
    rows = np.concatenate([np.asarray(a).transpose(0, 2, 1, 3).reshape(NPOOL * BLOCK, G * HD)
                           for a in (L0_cond_k_blocks, L0_cond_v_blocks)], axis=1)
    arrays = dict(
        xt=np.ascontiguousarray(xf.reshape(TILES, 128, C, 128).transpose(0, 3, 2, 1)),
        xtok=np.ascontiguousarray(xf),
        kvrows=rows,
        wkv=chunks(np.concatenate([np.asarray(L0_cond_Wk), np.asarray(L0_cond_Wv)], axis=0).T),
        wq=chunks(wq.transpose(0, 1, 3, 2, 4).reshape(D, 512)),
        wo=chunks(wo.transpose(0, 2, 1, 3, 4).reshape(512, D)),
        qs=np.asarray(L0_cond_q_norm_scale), ks=np.asarray(L0_cond_k_norm_scale),
        w1=np.asarray(L1_cond_weights),
        wb=chunks(np.asarray(L2_cond_W_base).T),
        wt=chunks(L2_cond_Wt),
        a2t=chunks(np.asarray(L2_cond_A).reshape(NE2 * RANK, D).T),
        b2t=chunks(np.asarray(L2_cond_B_w).transpose(1, 0, 2).reshape(D, NE2 * RANK)),
        wpt=chunks(np.asarray(L2_cond_Wp).T),
        s2=np.repeat(np.asarray(L2_cond_scaling), RANK)[:, None],
        w3=chunks(np.asarray(L3_cond_W).T),
        a3t=chunks(np.asarray(L3_cond_A).reshape(NE3 * RANK, D).T),
        b3t=np.ascontiguousarray(np.asarray(L3_cond_Bm).transpose(0, 2, 1).reshape(NE3 * RANK, D)),
        s3=np.repeat(np.asarray(L3_cond_scalings), RANK)[:, None],
        table=np.asarray(itok_Bx257_0_4111), kvl=np.asarray(itok_B_37_3939),
        subj=np.asarray(itok_B_0_7).reshape(TILES, 1, 2),
        ad2=np.asarray(itok_B_0_3), ad3=np.asarray(itok_B_0_6),
        const=constants(),
    )
    arrays = {n: np.ascontiguousarray(a) for n, a in arrays.items()}
    nc = bacc.Bacc("TRN2", target_bir_lowering=False, num_devices=1)
    args = {n: nc.dram_tensor(n + "_dram", a.shape, mybir.dt.from_np(a.dtype), kind="ExternalInput").ap()
            for n, a in arrays.items()}
    out = nc.dram_tensor("out_dram", (TILES, 128, D), mybir.dt.float32, kind="ExternalOutput").ap()
    build(nc, out=out, **args)
    r = run_bass_kernel_spmd(nc, [{n + "_dram": a for n, a in arrays.items()}], core_ids=[0])
    return r.results[0]["out_dram"].reshape(NB, NT, D)
```

```python
import concourse.bass as bass
from concourse import mybir
from contextlib import ExitStack
import numpy as np

NB, NT, D = 32, 64, 512
G, HD = 4, 64
BLOCK, WINDOW, NSLOT = 16, 256, 257
NPOOL = 16 * NSLOT
TILES = NB // 2
C = D // 128
WS = 21
NW = 5
WK = WS * BLOCK
CH = 3
KP = WK // CH
SP_ = KP // BLOCK
NE2, NE3, RANK = 4, 8, 16
NONE = 4096
NEG = 1.0e30

_WIDTHS = [[("ident", 128), ("diff", WK), ("negc", WK), ("inv", 32), ("tpos", 1), ("e2", 1), ("e3", 1),
            ("win", 1), ("toff", NW * BLOCK), ("code", 1)],
           [("order", NW * NW * NB), ("off", 1),
            ("spread", SP_ * KP), ("ones", NB)]]
CONST, NCONST = {}, [0, 0]
for _k in range(2):
    for _n, _w in _WIDTHS[_k]:
        CONST[_n] = (_k, NCONST[_k], _w)
        NCONST[_k] += _w


def constants():
    t = [np.zeros((rows, n), np.float32) for rows, n in zip((128, NB), NCONST)]

    def put(name, a):
        k, c, w = CONST[name]
        t[k][:a.shape[0], c:c + w] = a.reshape(a.shape[0], w)

    p = np.arange(128)
    put("ident", np.eye(128))
    put("diff", np.arange(WK)[None, :] - (p % NT)[:, None])
    put("negc", np.broadcast_to(-10000.0 * np.arange(WK), (128, WK)))
    inv = np.float32(1.0) / (np.float32(10000.0) ** (np.arange(32, dtype=np.float32) / np.float32(32)))
    put("inv", np.broadcast_to(inv.astype(np.float32), (128, 32)))
    put("tpos", (p % NT)[:, None])
    put("e2", (p // RANK)[:, None])
    put("e3", (p // RANK)[:, None])
    put("win", (NSLOT * np.arange(NB))[:, None])
    b = np.arange(NB)
    j = np.arange(NW)
    put("order", (NW * (b[:, None, None, None] - b[None, None, None, :]) + j[None, :, None, None] - j[None, None, :, None] > 0))
    put("toff", np.broadcast_to(np.arange(NW * BLOCK), (NB, NW * BLOCK)))
    put("code", (NT * b + 1)[:, None])
    put("off", np.arange(BLOCK)[:, None])
    q = np.arange(KP)
    put("spread", (q[None, None, :] == BLOCK * np.arange(SP_)[None, :, None] + np.arange(BLOCK)[:, None, None]))
    put("ones", np.ones((NB, NB)))
    return t


class Tile:

    def __init__(self, j, c):
        self.j, self.c = j, c

    def n(self, per, plus):
        return self.j * (2 * per) + (per * self.c + plus)

    def part(self, u):
        return 2 * self.c + u

    def b(self, u, per, plus):
        return self.j * (4 * per) + (per * self.part(u) + plus)

    def ring(self, u):
        q, r = divmod(self.part(u), 4)
        return r, self.j * 48 + 48 * (q + 1)


def after(eng, sem, value):
    if not isinstance(value, int) or value > 0:
        eng.wait_ge(sem, value)


def build(nc, xt, xtok, kvrows, wkv, wq, wo, qs, ks, w1, wb, wt, a2t, b2t, wpt, s2, w3, a3t, b3t, s3,
          table, kvl, subj, ad2, ad3, const, constf, out):
    f32, i32, f16 = mybir.dt.float32, mybir.dt.int32, mybir.dt.float16
    ALU, ACT, AX = mybir.AluOpType, mybir.ActivationFunctionType, mybir.AxisListType.X
    ctx = ExitStack()
    with ctx:
        def sb(name, shape, dt=f32):
            return ctx.enter_context(nc.sbuf_tensor(name, shape, dt))

        def sem(name):
            return ctx.enter_context(nc.semaphore(name))

        newkv = nc.dram_tensor("newkv", [NB * NT + 1, 2 * G * HD], f32).ap()
        newkv_t = newkv[1:NB * NT + 1, :].rearrange("(n p) f -> n p f", p=128)

        cst = [sb("cst", [128, NCONST[0]]), sb("cst_few", [NB, NCONST[1]])]

        def con(name, rows=128):
            k, c, w = CONST[name]
            return cst[k][0:rows, c:c + w]

        ident = con("ident")
        wkv_s = sb("wkv_s", [128, C, 512])
        wq_s = sb("wq_s", [128, C, 512])
        wo_s = sb("wo_s", [128, C, 512])
        wb_s = sb("wb_s", [128, C, 512])
        w3_s = sb("w3_s", [128, C, 512])
        wide = sb("wide", [128, 2, C, 512])
        wt_s, wpt_s = wide[:, 0], wide[:, 1]
        flat = wide[:].rearrange("p a c n -> p (a c n)")
        prob = [flat[:, G * WK * i:G * WK * (i + 1)].rearrange("p (g k) -> p g k", g=G) for i in range(2)]
        neg_s = flat[:, 2 * G * WK:3 * G * WK].rearrange("p (g k) -> p g k", g=G)
        windows = sb("windows", [128, 4 * CH * 512])
        kv_s = [windows[0:KP, CH * 512 * i:CH * 512 * (i + 1)].rearrange("p (c n) -> p c n", c=CH) for i in range(4)]
        same = windows[0:NB, 0:NW * WS * NB // 2].bitcast(f16).rearrange("p (j n) -> p j n", j=NW)
        rows = windows[0:BLOCK, NW * WS * NB:(NW + 2) * WS * NB].rearrange("p (k n) -> p k n", k=2)
        a2_s = sb("a2_s", [128, C, 64])
        b2_s = sb("b2_s", [128, C, 64])
        a3_s = sb("a3_s", [128, C, 128])
        b3_s = sb("b3_s", [128, 512])
        down2 = sb("down2", [128, C, 64])
        up2 = sb("up2", [128, 512])
        scl2, scl3 = sb("scl2", [128, 1]), sb("scl3", [128, 1])
        idx2, idx3 = sb("idx2", [128, NB], i32), sb("idx3", [128, NB], i32)
        pick2, pick3 = sb("pick2", [128, NB]), sb("pick3", [128, NB])
        kvb = sb("kvb", [128, NB], i32)
        kvi = sb("kvi", [128, NB], i32)
        k0f, r0f = sb("k0f", [128, NB]), sb("r0f", [128, NB])
        band = sb("band", [128, NB])
        limit = sb("limit", [128, NB])
        start = sb("start", [128, NB])
        pos = sb("pos", [128, TILES])
        ang = sb("ang", [128, TILES, 32])
        turns = sb("turns", [128, TILES, 32])
        rest = sb("rest", [128, TILES, 32])
        sinx = sb("sinx", [128, TILES, 32])
        nsinx = sb("nsinx", [128, TILES, 32])
        cosx = sb("cosx", [128, TILES, 32])
        nscale = {"q": sb("qscale", [128, 64]), "k": sb("kscale", [128, 64])}
        costab = {"q": sb("qcos", [128, TILES, 64]), "k": sb("kcos", [128, TILES, 64])}
        sintab = {"q": sb("qsin", [128, TILES, 64]), "k": sb("ksin", [128, TILES, 64])}
        kvc = sb("kvc", [NB, 2], i32)
        kvcf = sb("kvcf", [NB, 3])
        first_slot = sb("first_slot", [NB, 1], i32)
        blk_i = sb("blk_i", [NB, WS], i32)
        blk = sb("blk", [NB, WS])
        blkd = sb("blkd", [NB, WS, NB])
        blkrow = sb("blkrow", [NB, WS, NB])
        later = sb("later", [NB, NW, NW * NB], f16)
        wt_tok = sb("wt_tok", [NB, NW * BLOCK])
        wt_ge = sb("wt_ge", [NB, NW * BLOCK])
        cover = sb("cover", [NB, NW * BLOCK], f16)
        code = sb("code", [NB, NW * BLOCK])
        wcode = sb("wcode", [NB, NW * BLOCK], f16)
        none = sb("none", [BLOCK, WS * NB])
        down_t = sb("down_t", [64, 512])
        idx_all = sb("idx_all", [KP, NB, 2 * CH], i32)
        idx_b = [sb(f"idx_b{i}", [KP, 2 * CH], i32) for i in range(2)]
        xt_s = [sb(f"xt_s{i}", [128, C, 128]) for i in range(4)]
        kvo = [sb(f"kvo{i}", [128, 512]) for i in range(2)]
        nr = {}
        for w, h in (("q", 8), ("k", 4)):
            nr[w] = dict(sq=sb(w + "_sq", [128, h, 64]), ss=sb(w + "_ss", [128, h]), ms=sb(w + "_ms", [128, h]),
                         rstd=sb(w + "_rstd", [128, h]), n=sb(w + "_n", [128, h, 64]), t1=sb(w + "_t1", [128, h, 64]),
                         t2=sb(w + "_t2", [128, h, 64]))
        half = sb("half", [128, 8])
        kt_s = sb("kt_s", [128, 2, WK])
        qrot = sb("qrot", [128, 512])
        qz = sb("qz", [128, 2, 512])
        mask = [sb(f"mask{i}", [128, WK]) for i in range(2)]
        negmax = sb("negmax", [128, G])
        psum_p = [sb(f"psum_p{i}", [128, G]) for i in range(2)]
        rinv = [sb(f"rinv{i}", [128, G]) for i in range(2)]
        pt_s = [sb(f"pt_s{i}", [KP, CH, 128]) for i in range(G)]
        ot_s = sb("ot_s", [128, 4, 128])
        xtok_s = sb("xtok_s", [128, 512])
        x1 = sb("x1", [128, 512])
        w1raw = sb("w1raw", [128, 128])
        w1i = sb("w1i", [128, 128])
        x2t = sb("x2t", [128, C, 128])
        x3t = sb("x3t", [128, C, 128])
        z2m = sb("z2m", [128, 128])
        z3m = sb("z3m", [128, 128])
        xo = sb("xo", [128, 512])
        subj_s = sb("subj_s", [1, 2], i32)

        gb = [ctx.enter_context(nc.psum_tensor(f"gb{i}", [128, 512], f32)) for i in range(2)]
        sbk = [ctx.enter_context(nc.psum_tensor(f"sbk{i}", [128, 512], f32)) for i in range(2)]
        tb = [ctx.enter_context(nc.psum_tensor(f"tb{i}", [128, 512], f32)) for i in range(2)]
        ob = [ctx.enter_context(nc.psum_tensor(f"ob{i}", [128, 512], f32)) for i in range(2)]

        names = """row0_stored l_const l_few l_table l_kvc l_kv l_scale l_wq l_wo l_wb l_w3 l_low3 l_up l_ad
            set_dve blk_ready zeroed tab_ready sin_done slot_ready scale_ready qtab_ready
            blkd_ready blkrow_mm blkrow_ev covered later_ready lose_mm  wcode_ready win_mm rows_ready
            idx_mm idx_ready down_mm down_ev downt_mm downt_ev up_mm up_ev w_ident
            ka_mm k_sq k_copied k_ss k_ms k_rstd k_t2 k_n k_rot
            q_mm q_sq q_ss q_ms q_rstd q_n q_t2 q_rot qt_mm qz_ready l_xq
            kt_mm kt_ev s_mm mask_band mask_start mask_ready negs_ready exp_done rinv_ready prob_ready
            pt_mm pt_ev pv_mm ot_ev idx_copied
            wo_mm x1_ready l_xtok l_subj l_w1 w1i_ready l1_mm x2_ready z2_mm z2_ready x3_mm x3_ready
            z3_mm z3_ready out_mm xo_ready stored""".split()
        S = {n: sem(n) for n in names}
        l_wkv = [sem(f"l_wkv{i}") for i in range(C)]
        l_xt = [sem(f"l_xt{i}") for i in range(4)]
        kv_stored = [sem(f"kv_stored{i}") for i in range(2)]
        kv_old = [sem(f"kv_old{i}") for i in range(4)]
        kv_new = [sem(f"kv_new{i}") for i in range(4)]
        block = ctx.enter_context(nc.Block())

        def wait_alone(eng, *waits):
            waits = [(sem, v if isinstance(v, int) else eng.snap(eng.to_reg(v)))
                     for sem, v in waits if not isinstance(v, int) or v > 0]
            if waits:
                eng.wait_ge(S["l_const"], 16)
                for sem, v in waits:
                    eng.wait_ge(sem, v)

        HALF_A = TILES // 2

        def tables(eng, w):
            lo, hi = (nscale[w][:, 32 * a:32 * a + 32].unsqueeze(1).to_broadcast([128, TILES, 32]) for a in (0, 1))
            return [eng.tensor_tensor(costab[w][:, :, 0:32], cosx[:], lo, ALU.mult),
                    eng.tensor_tensor(costab[w][:, :, 32:64], cosx[:], hi, ALU.mult),
                    eng.tensor_tensor(sintab[w][:, :, 32:64], sinx[:], lo, ALU.mult),
                    eng.tensor_tensor(sintab[w][:, :, 0:32], nsinx[:], hi, ALU.mult)]

        @block.sync
        def _(sp):
            def load_xt(n, i):
                sp.dma_start(xt_s[i][:], xt[n]).then_inc(l_xt[i], 16)

            load_xt(0, 0)
            for c in range(C):
                sp.dma_start(wkv_s[:, c], wkv[:, c]).then_inc(l_wkv[c], 16)
            for i in range(1, 4):
                load_xt(i, i)
            for w, src in (("q", qs), ("k", ks)):
                sp.dma_start(nscale[w][:], src.partition_broadcast(128)).then_inc(S["l_scale"], 16)

            def store_kv(n, i):
                sp.wait_ge(S["k_rot"], n + 1)
                sp.dma_start(newkv_t[n], kvo[i][:]).then_inc(kv_stored[i], 16)

            pieces = [(w[:, c], src[:, c], name) for w, src, name in
                      ((wq_s, wq, "l_wq"), (wb_s, wb, "l_wb"), (w3_s, w3, "l_w3"), (wt_s, wt, "l_up"), (wpt_s, wpt, "l_up"),
                       (wo_s, wo, "l_wo")) for c in range(C)]
            pieces += [(a2_s[:], a2t, "l_up"), (b2_s[:], b2t, "l_up"), (a3_s[:], a3t, "l_low3"), (b3_s[:], b3t, "l_low3")]
            each = -(-len(pieces) // (TILES - 4))
            for n in range(TILES):
                if n < TILES - 4:
                    sp.wait_ge(S["ka_mm"], n + 1)
                    load_xt(n + 4, n % 4)
                store_kv(n, n % 2)
                if n == 0:
                    sp.dma_start(ot_s[:], xt[0]).then_inc(S["l_xq"], 16)
                for dst, src, name in pieces[n * each:(n + 1) * each]:
                    sp.dma_start(dst, src).then_inc(S[name], 16)

            def load_xq(n, before):
                after(sp, S["q_mm"], before)
                sp.dma_start(xt_s[0][:], xt[n]).then_inc(S["l_xq"], 16)

            def tile(t, first, last):
                if not last:
                    load_xq(t.n(1, 1), t.n(1, 1))
                after(sp, S["x1_ready"], t.n(1, 0))
                sp.dma_start(xtok_s[:], xtok[t.n(1, 0)]).then_inc(S["l_xtok"], 16)
                sp.dma_start(subj_s[:], subj[t.n(1, 0)]).then_inc(S["l_subj"], 16)
                after(sp, S["w1i_ready"], t.n(1, 0))
                wait_alone(sp, (S["l_subj"], t.n(16, 16)))
                for u in range(2):
                    s = sp.value_load(subj_s[0:1, u:u + 1], min_val=0, max_val=7)
                    sp.dma_start(w1raw[64 * u:64 * u + 64, 64 * u:64 * u + 64], w1[s]).then_inc(S["l_w1"], 16)
                if not first:
                    sp.wait_ge(S["xo_ready"], t.n(1, 0))
                    sp.dma_start(out[t.n(1, -1)], xo[:]).then_inc(S["stored"], 16)

            sp.wait_ge(S["ka_mm"], TILES)
            sp.wait_ge(S["zeroed"], 1)
            tile(Tile(0, 0), True, False)
            with sp.Fori(0, TILES // 2 - 1) as j:
                for c in (1, 2):
                    tile(Tile(j, c), False, False)
            tile(Tile(TILES // 2 - 1, 1), False, True)
            sp.wait_ge(S["xo_ready"], TILES)
            sp.dma_start(out[TILES - 1], xo[:]).then_inc(S["stored"], 16)
            sp.wait_ge(S["stored"], 16 * (TILES + 1))

        @block.gpsimd
        def _(pool):
            nc.gpsimd.dma_start(kvc[:, 0:1], kvl.rearrange("(b a) -> b a", a=1)).then_inc(S["l_kvc"], 16)
            nc.gpsimd.memset(half[:], -0.5)
            nc.gpsimd.memset(qz[:], 0.0)
            nc.gpsimd.memset(up2[:], 0.0)
            nc.gpsimd.memset(z2m[:], 0.0)
            nc.gpsimd.memset(w1raw[:], 0.0).then_inc(S["zeroed"], 1)
            pool.wait_ge(S["zeroed"], 1)
            nc.gpsimd.dma_start(newkv[0:1, :], up2[127:128, :]).then_inc(S["row0_stored"], 16)

            def root(w, h, value):
                pool.wait_ge(S[w + "_ms"], value)
                nc.gpsimd.tensor_tensor(nr[w]["rstd"][:], nr[w]["ms"][:], half[:, 0:h], ALU.pow).then_inc(S[w + "_rstd"], 1)

            P = nc.gpsimd
            pool.wait_ge(S["slot_ready"], 1)
            P.indirect_dma_start(blk_i[:], None, table, bass.IndirectOffsetOnAxis(ap=first_slot[:], axis=0),
                                 bounds_check=NB * NSLOT - WS, oob_is_err=False).then_inc(S["l_table"], 16)
            pool.wait_ge(S["l_table"], 16)
            P.tensor_copy(blk[:], blk_i[:]).then_inc(S["blk_ready"], 1)
            pool.wait_ge(S["blk_ready"], 1)
            pool.wait_ge(S["l_const"], 16)
            P.tensor_tensor(blkd[:], blk[:].unsqueeze(2).to_broadcast([NB, WS, NB]),
                            con("ident", NB)[:, 0:NB].unsqueeze(1).to_broadcast([NB, WS, NB]), ALU.mult).then_inc(S["blkd_ready"], 1)
            for n in range(4):
                root("k", 4, n + 1)
            pool.wait_ge(S["scale_ready"], 1)
            pool.wait_ge(S["sin_done"], 1)
            tables(P, "q")[-1].then_inc(S["qtab_ready"], 1)
            for n in range(4, HALF_A):
                root("k", 4, n + 1)
            for name, w in (("l_wb", wb_s), ("l_w3", w3_s)):
                pool.wait_ge(S[name], 16 * C)
                for c in range(C):
                    d = w[:, c, 128 * c:128 * c + 128]
                    last = nc.gpsimd.tensor_tensor(d, d, ident, ALU.add)
            last.then_inc(S["w_ident"], 1)
            root("q", 8, 1)

            def copy_index(t, u, k):
                i = (t.part(u) + k) % 2
                n = t.b(u, 1, k)
                src = idx_all[:, n:n + 1, :] if isinstance(n, int) else idx_all[:, bass.ds(n, 1), :]
                nc.gpsimd.tensor_copy(idx_b[i][:], src.rearrange("p a k -> p (a k)")).then_inc(S["idx_copied"], 1)

            def gather(t, u, k, new):
                r, done = t.ring(u + k)
                i = (t.part(u) + k) % 2
                for c in range(CH):
                    nc.gpsimd.indirect_dma_start(
                        kv_s[r][:, c, :], None, newkv if new else kvrows,
                        bass.IndirectOffsetOnAxis(ap=idx_b[i][:, new * CH + c:new * CH + c + 1], axis=0),
                        bounds_check=NB * NT if new else NPOOL * BLOCK - 1, oob_is_err=False,
                    ).then_inc((kv_new if new else kv_old)[r], 16)

            t0 = Tile(0, 0)

            def gather_first(k):
                copy_index(t0, 0, k)
                pool.wait_ge(S["idx_copied"], k + 1)
                gather(t0, 0, k, 0)

            pool.wait_ge(S["idx_ready"], 1)
            gather_first(0)
            with pool.Fori(HALF_A, TILES) as i:
                root("k", 4, i + 1)

            def lay_over(t, u, k):
                r, done = t.ring(u + k)
                wait_alone(pool, (kv_old[r], done))
                gather(t, u, k, 1)

            def norm(t, u, k):
                i = (t.part(u) + k) % 2
                for g in range(G):
                    wait_alone(pool, (S["rinv_ready"], t.b(u, 2, 2 * k + g // 2 + 1)))
                    nc.gpsimd.tensor_scalar(prob[i][:, g, :], prob[i][:, g, :], rinv[i][:, g:g + 1], 1.0,
                                            ALU.mult, ALU.mult).then_inc(S["prob_ready"], 1)

            def w1_ident(t):
                pool.wait_ge(S["l_w1"], t.n(32, 32))
                after(pool, S["l1_mm"], t.n(1, 0))
                nc.gpsimd.tensor_tensor(w1i[:], w1raw[:], ident, ALU.add).then_inc(S["w1i_ready"], 1)

            def slot(t, u, b_left):
                if u == 1 and b_left > 0:
                    root("q", 8, t.n(1, 2))
                if b_left >= 3:
                    r, done = t.ring(u + 1)
                    pool.wait_ge(kv_new[r], done)
                    copy_index(t, u, 3)
                    wait_alone(pool, (S["idx_copied"], t.b(u, 1, 4)), (S["pv_mm"], t.b(u, 2, 0)))
                    gather(t, u, 3, 0)
                if b_left >= 2:
                    lay_over(t, u, 2)
                if u == 1:
                    w1_ident(t)
                if b_left >= 1:
                    norm(t, u, 1)

            gather_first(1)
            pool.wait_ge(S["row0_stored"], 16)
            for i in range(2):
                pool.wait_ge(kv_stored[i], 16 * TILES // 2)
            for k in range(2):
                lay_over(t0, 0, k)
            r, done = t0.ring(0)
            pool.wait_ge(kv_new[r], done)
            copy_index(t0, 0, 2)
            pool.wait_ge(S["idx_copied"], 3)
            gather(t0, 0, 2, 0)
            norm(t0, 0, 0)
            slot(t0, 0, NB - 1)
            slot(t0, 1, NB - 2)
            with pool.Fori(0, TILES // 2 - 2) as j:
                for c in (1, 2):
                    for u in range(2):
                        slot(Tile(j, c), u, 3)
            for c in (1, 2, 3):
                for u in range(2):
                    slot(Tile(TILES // 2 - 2, c), u, 2 * (3 - c) + 1 - u)

        @block.scalar
        def _(act):
            act.dma_start(kvb[:], kvl.partition_broadcast(128)).then_inc(S["l_kv"], 16)
            act.dma_start(cst[0][:], const).then_inc(S["l_const"], 16)
            act.dma_start(cst[1][:], constf).then_inc(S["l_few"], 16)
            for d, s in ((scl2[0:64], s2), (scl3[:], s3), (idx2[:], ad2.partition_broadcast(128)),
                         (idx3[:], ad3.partition_broadcast(128))):
                act.dma_start(d, s).then_inc(S["l_ad"], 16)
            act.wait_ge(S["tab_ready"], 1)
            nc.scalar.activation(sinx[:], rest[:], ACT.Sin)
            nc.scalar.activation(nsinx[:], rest[:], ACT.Sin, scale=-1.0)
            nc.scalar.activation(cosx[:], turns[:], ACT.Sin).then_inc(S["sin_done"], 1)

            def key_tile(n, i, free):
                act.wait_ge(S["ka_mm"], n + 1)
                after(act, S["k_ss"], n)
                nc.scalar.activation(nr["k"]["sq"][:], gb[i][:, 0:256].rearrange("p (g d) -> p g d", g=G),
                                     ACT.Square).then_inc(S["k_sq"], 1)
                after(act, kv_stored[i], free)
                nc.scalar.activation(kvo[i][:], gb[i][:], ACT.Copy).then_inc(S["k_copied"], 1)

            def square(n, bank):
                act.wait_ge(S["q_mm"], n)
                nc.scalar.activation(nr["q"]["sq"][:], bank[:].rearrange("p (h d) -> p h d", h=8),
                                     ACT.Square).then_inc(S["q_sq"], 1)

            def queries(n, used, bank):
                act.wait_ge(S["qt_mm"], n)
                after(act, S["s_mm"], used)
                for h in range(2):
                    nc.scalar.activation(qz[64 * h:64 * h + 64, h], bank[64 * h:64 * h + 64, :],
                                         ACT.Copy).then_inc(S["qz_ready"], 1)

            for n in range(4):
                key_tile(n, n % 2, 16 * (n // 2))
            HW = WS * NB // 2

            def evac(dst, src, ready, done):
                act.wait_ge(S[ready], 1)
                nc.scalar.activation(dst, src, ACT.Copy).then_inc(S[done], 1)
            brow = blkrow[:].rearrange("p s b -> p (s b)")
            for i in range(2):
                evac(brow[:, HW * i:HW * i + HW], ob[i][0:NB, 0:HW], "blkrow_mm", "blkrow_ev")
            for n in range(4, HALF_A):
                key_tile(n, n % 2, 16 * (n // 2))
            square(1, sbk[0])
            evac(idx_all[:], tb[0][0:KP, 0:2 * CH * NB].rearrange("p (k b) -> p b k", b=NB), "idx_mm", "idx_ready")
            with act.Fori(HALF_A // 2, TILES // 2) as j:
                for i in range(2):
                    key_tile(j * 2 + i, i, j * 16)
            act.wait_ge(S["zeroed"], 1)
            queries(1, 0, sbk[1])
            evac(down_t[:], tb[1][0:64, :], "down_mm", "down_ev")
            evac(up2[0:64, :], ob[0][0:64, :], "up_mm", "up_ev")
            evac(down2[:], ob[1][:, 0:C * 64].rearrange("p (c r) -> p c r", c=C), "downt_mm", "downt_ev")

            def exps(t, u, k, g):
                i = (t.part(u) + k) % 2
                act.wait_ge(S["negs_ready"], t.b(u, 4, 4 * k + g + 1))
                after(act, S["pt_mm"], t.b(u, 4, 4 * (k - 2) + g + 1))
                nc.scalar.activation(prob[i][:, g, :], neg_s[:, g, :], ACT.Exp, bias=negmax[:, g:g + 1], scale=-1.0,
                                     accum_out=psum_p[i][:, g:g + 1]).then_inc(S["exp_done"], 1)

            def probs_t(t, u, g):
                act.wait_ge(S["pt_mm"], t.b(u, 4, g + 1))
                after(act, S["pv_mm"], t.b(u, 2, g // 2 - 1))
                nc.scalar.activation(pt_s[g][:], tb[g % 2][0:KP, 0:CH * 128].rearrange("p (c q) -> p c q", c=CH),
                                     ACT.Copy).then_inc(S["pt_ev"], 1)

            def attn_out(t, u):
                act.wait_ge(S["pv_mm"], t.b(u, 2, 2))
                after(act, S["wo_mm"], t.n(1, 0))
                nc.scalar.activation(ot_s[:, :, 64 * u:64 * u + 64],
                                     ob[u][:, 0:256].rearrange("p (k t) -> p k t", k=4), ACT.Copy).then_inc(S["ot_ev"], 1)

            def evac(src, dst, ready, value, done):
                act.wait_ge(S[ready], value)
                nc.scalar.activation(dst, src, ACT.Copy).then_inc(S[done], 1)

            def layer1(t):
                evac(gb[1][:].rearrange("p (c t) -> p c t", c=C), x2t[:], "l1_mm", t.n(1, 0), "x2_ready")

            def layer2(t):
                evac(gb[1][:].rearrange("p (c t) -> p c t", c=C), x3t[:], "x3_mm", t.n(1, 0), "x3_ready")

            def layer3(t):
                act.wait_ge(S["out_mm"], t.n(1, 0))
                act.wait_ge(S["stored"], t.n(16, 0))
                nc.scalar.activation(xo[:], gb[0][:], ACT.Copy).then_inc(S["xo_ready"], 1)

            def tile(t, first, last):
                exps(t, 0, 1, 0)
                probs_t(t, 0, 0)
                exps(t, 0, 1, 1)
                probs_t(t, 0, 1)
                exps(t, 0, 1, 2)
                exps(t, 0, 1, 3)
                if not last:
                    square(t.n(1, 2), gb[0])
                if not first:
                    layer1(t)
                probs_t(t, 0, 2)
                probs_t(t, 0, 3)
                if not first:
                    layer2(t)
                attn_out(t, 0)
                if not last:
                    queries(t.n(1, 2), t.b(1, 4, 4), gb[1])
                if not first:
                    layer3(t)
                probs_t(t, 1, 0)
                probs_t(t, 1, 1)
                if not last:
                    exps(t, 1, 1, 0)
                    exps(t, 1, 1, 1)
                probs_t(t, 1, 2)
                probs_t(t, 1, 3)
                if not last:
                    exps(t, 1, 1, 2)
                attn_out(t, 1)
                if not last:
                    exps(t, 1, 1, 3)

            act.sem_inc(S["stored"], 16)
            for g in range(G):
                exps(Tile(0, 0), 0, 0, g)
            tile(Tile(0, 0), True, False)
            with act.Fori(0, TILES // 2 - 1) as j:
                for c in (1, 2):
                    tile(Tile(j, c), False, False)
            tile(Tile(TILES // 2 - 1, 1), False, True)
            end = Tile(TILES // 2, 0)
            layer1(end)
            layer2(end)
            layer3(end)

        @block.vector
        def _(dve):
            n_set = [0]

            def link(ins):
                n_set[0] += 1
                ins.then_inc(S["set_dve"], 1)
                dve.wait_ge(S["set_dve"], n_set[0])

            V = nc.vector
            dve.wait_ge(S["l_kvc"], 16)
            link(V.tensor_scalar(kvc[:, 1:2], kvc[:, 0:1], 4, None, ALU.arith_shift_right))
            V.tensor_copy(kvcf[:, 1:2], kvc[:, 0:1])
            link(V.tensor_copy(kvcf[:, 0:1], kvc[:, 1:2]))
            dve.wait_ge(S["l_const"], 16)
            link(V.tensor_tensor(kvcf[:, 2:3], kvcf[:, 0:1], con("win", NB), ALU.add))
            V.tensor_copy(first_slot[:], kvcf[:, 2:3]).then_inc(S["slot_ready"], 1)
            link(V.scalar_tensor_tensor(kvcf[:, 1:2], kvcf[:, 0:1], -16.0, kvcf[:, 1:2], ALU.mult, ALU.add))
            link(V.tensor_scalar(wt_tok[:], con("toff", NB), kvcf[:, 1:2], None, ALU.subtract))
            link(V.tensor_scalar(wt_ge[:], wt_tok[:], 0.0, None, ALU.is_ge))
            link(V.scalar_tensor_tensor(cover[:], wt_tok[:], float(NT), wt_ge[:], ALU.is_lt, ALU.mult))
            V.scalar_tensor_tensor(code[:], wt_tok[:], con("code", NB), cover[:], ALU.add, ALU.mult).then_inc(S["covered"], 1)
            dve.wait_ge(S["l_kv"], 16)
            V.tensor_scalar(kvi[:], kvb[:], 4, None, ALU.arith_shift_right)
            V.tensor_copy(pos[0:64, :], kvb[0:64].rearrange("p (n u) -> p n u", u=2)[:, :, 0])
            link(V.tensor_copy(pos[64:128, :], kvb[64:128].rearrange("p (n u) -> p n u", u=2)[:, :, 1]))
            link(V.tensor_copy(k0f[:], kvi[:]))
            V.tensor_copy(r0f[:], kvb[:])
            link(V.tensor_scalar(pos[:], pos[:], con("tpos"), None, ALU.add))
            V.scalar_tensor_tensor(r0f[:], k0f[:], -16.0, r0f[:], ALU.mult, ALU.add)
            inv = con("inv").unsqueeze(1).to_broadcast([128, TILES, 32])
            link(V.tensor_tensor(ang[:], pos[:].unsqueeze(2).to_broadcast([128, TILES, 32]), inv, ALU.mult))
            MAGIC = 1.5 * 2.0 ** 23
            link(V.tensor_scalar(turns[:], ang[:], float(1.0 / (2.0 * np.pi)), MAGIC, ALU.mult, ALU.add))
            link(V.tensor_scalar(turns[:], turns[:], -MAGIC, None, ALU.add))
            c1 = 6.28125
            c2 = float(np.float32(np.round((2 * np.pi - c1) * 2.0 ** 22) / 2.0 ** 22))
            c3 = float(np.float32(2 * np.pi - c1 - c2))
            link(V.scalar_tensor_tensor(rest[:], turns[:], -c1, ang[:], ALU.mult, ALU.add))
            link(V.scalar_tensor_tensor(rest[:], turns[:], -c2, rest[:], ALU.mult, ALU.add))
            link(V.scalar_tensor_tensor(rest[:], turns[:], -c3, rest[:], ALU.mult, ALU.add))
            link(V.tensor_scalar(rest[:], rest[:], 3.1415925, -3.1415925, ALU.min, ALU.max))
            link(V.scalar_tensor_tensor(turns[:], rest[:], -1.0, rest[:], ALU.mult, ALU.max))
            V.tensor_scalar(turns[:], turns[:], -1.0, float(np.pi / 2), ALU.mult, ALU.add).then_inc(S["tab_ready"], 1)
            dve.wait_ge(S["l_scale"], 32)
            V.tensor_scalar(nscale["q"][:], nscale["q"][:], 1.0, None, ALU.add)
            V.tensor_scalar(nscale["k"][:], nscale["k"][:], 1.0, None, ALU.add).then_inc(S["scale_ready"], 1)
            dve.wait_ge(S["scale_ready"], 1)
            dve.wait_ge(S["sin_done"], 1)
            link(tables(V, "k")[-1])

            def norm_rotate(w, h, src, dst, tab, value, gate=None, between=None):
                def done(step):
                    return S[w + "_" + step]
                k = nr[w]
                dve.wait_ge(done("sq"), value)
                V.reduce_sum(k["ss"][:], k["sq"][:], AX).then_inc(done("ss"), 1)
                dve.wait_ge(done("ss"), value)
                V.tensor_scalar(k["ms"][:], k["ss"][:], 1.0 / HD, 1e-6, ALU.mult, ALU.add).then_inc(done("ms"), 1)
                cos, sin = (x[w][:, tab:tab + 1, :] if isinstance(tab, int) else x[w][:, bass.ds(tab, 1), :] for x in (costab, sintab))
                if w == "k":
                    dve.wait_ge(S["k_copied"], value)
                V.tensor_tensor(k["t1"][:], src, cos.to_broadcast([128, h, 64]), ALU.mult)
                V.tensor_tensor(k["t2"][:, :, 0:32], src[:, :, 32:64], sin[:, :, 0:32].to_broadcast([128, h, 32]), ALU.mult)
                V.tensor_tensor(k["t2"][:, :, 32:64], src[:, :, 0:32], sin[:, :, 32:64].to_broadcast([128, h, 32]),
                                ALU.mult).then_inc(done("t2"), 1)
                dve.wait_ge(done("t2"), value)
                V.tensor_tensor(k["n"][:], k["t1"][:], k["t2"][:], ALU.add).then_inc(done("n"), 1)
                if between:
                    between()
                if gate:
                    gate()
                dve.wait_ge(done("rstd"), value)
                dve.wait_ge(done("n"), value)
                V.tensor_tensor(dst, k["n"][:], k["rstd"][:].unsqueeze(2).to_broadcast([128, h, 64]),
                                ALU.mult).then_inc(done("rot"), 1)

            def key_tile(n, i):
                k = kvo[i][:, 0:256].rearrange("p (g d) -> p g d", g=G)
                norm_rotate("k", 4, k, k, n, n + 1)

            with dve.Fori(0, HALF_A // 4) as j:
                for i in range(2):
                    key_tile(j * 2 + i, i)
            dve.wait_ge(S["blkrow_ev"], 2)
            brow = blkrow[:].rearrange("p s b -> p (s b)")
            for j in range(NW):
                last = V.tensor_scalar(same[:, j, :], brow, blk[:, WS - NW + j:WS - NW + j + 1], None, ALU.is_equal)
            link(last)
            dve.wait_ge(S["l_few"], 16)
            V.tensor_tensor(later[:], same[:, :, (WS - NW) * NB:], con("order", NB).rearrange("p (j e) -> p j e", j=NW),
                            ALU.mult).then_inc(S["later_ready"], 1)
            V.tensor_scalar(rows[:, 0, :], brow[0:BLOCK], float(BLOCK), con("off", BLOCK), ALU.mult, ALU.add)
            with dve.Fori(HALF_A // 4, HALF_A // 2) as j:
                for i in range(2):
                    key_tile(j * 2 + i, i)
            dve.wait_ge(S["lose_mm"], 1)
            V.scalar_tensor_tensor(wcode[:], tb[0][0:NB, 0:NW * BLOCK], 0.0, code[:], ALU.is_equal, ALU.mult).then_inc(S["wcode_ready"], 1)
            HW = WS * NB // 2
            dve.wait_ge(S["win_mm"], 1)
            for i in range(2):
                w = ob[i][0:BLOCK, 0:HW]
                link(V.tensor_scalar(none[:, HW * i:HW * i + HW], w, 0.0, float(NONE), ALU.is_equal, ALU.mult))
                last = V.tensor_tensor(rows[:, 1, HW * i:HW * i + HW], w, none[:, HW * i:HW * i + HW], ALU.add)
            last.then_inc(S["rows_ready"], 1)

            V.tensor_scalar(band[:], r0f[:], 2.0, WINDOW + 1.0, ALU.mult, ALU.add)
            V.tensor_scalar(start[:], k0f[:], -160000.0, 2555000.0, ALU.mult, ALU.add)
            link(V.tensor_scalar(limit[:], r0f[:], -1.0, -WINDOW - 0.5, ALU.mult, ALU.add))
            V.scalar_tensor_tensor(limit[:], r0f[:], 0.5, limit[:], ALU.add, ALU.mult)
            dve.wait_ge(S["l_ad"], 64)
            V.tensor_scalar(pick2[0:64], idx2[0:64], con("e2", 64), scl2[0:64], ALU.is_equal, ALU.mult)
            V.tensor_scalar(pick3[:], idx3[:], con("e3"), scl3[:], ALU.is_equal, ALU.mult)
            def query_tile(t, plus, between, bank):
                norm_rotate("q", 8, bank[:].rearrange("p (h d) -> p h d", h=8), qrot[:].rearrange("p (h d) -> p h d", h=8),
                            t.n(1, plus), t.n(1, plus + 1), between=between,
                            gate=lambda: after(dve, S["qt_mm"], t.n(1, plus)))

            dve.wait_ge(S["qtab_ready"], 1)
            query_tile(Tile(0, 0), 0, None, sbk[0])

            with dve.Fori(HALF_A // 2, TILES // 2) as j:
                for i in range(2):
                    key_tile(j * 2 + i, i)

            dve.wait_ge(S["zeroed"], 1)

            def make_mask(t, u, k):
                m = mask[(t.part(u) + k) % 2]
                n = t.b(u, 1, k)
                col = (lambda a: a[:, n:n + 1]) if isinstance(n, int) else (lambda a: a[:, bass.ds(n, 1)])
                V.scalar_tensor_tensor(m[:], con("diff"), col(band), con("diff"), ALU.subtract, ALU.mult).then_inc(S["mask_band"], 1)
                dve.wait_ge(S["mask_band"], t.b(u, 1, k + 1))
                V.scalar_tensor_tensor(m[:], con("negc"), col(start), m[:], ALU.add, ALU.max).then_inc(S["mask_start"], 1)
                dve.wait_ge(S["mask_start"], t.b(u, 1, k + 1))
                V.tensor_scalar(m[:], m[:], col(limit), -NEG, ALU.is_gt, ALU.mult).then_inc(S["mask_ready"], 1)

            def keys_t(t, u, k):
                for p in range(2):
                    dve.wait_ge(S["kt_mm"], t.b(u, 2, 2 * k + p + 1))
                    after(dve, S["s_mm"], t.b(u, 4, 4 * k - 2 + 2 * p))
                    V.tensor_copy(kt_s[:, p, :], tb[p][:, 0:WK]).then_inc(S["kt_ev"], 1)

            def scores(t, u, k):
                dve.wait_ge(S["mask_ready"], t.b(u, 1, k + 1))
                for g in range(G):
                    wait_alone(dve, (S["s_mm"], t.b(u, 4, 4 * k + g + 1)),
                               (S["exp_done"], t.b(u, 4, 4 * (k - 1) + g + 1)))
                    V.tensor_tensor_reduce(out=neg_s[:, g, :], in0=sbk[g % 2][:, 0:WK], in1=mask[(t.part(u) + k) % 2][:],
                                           scale=-1.0 / 16, scalar=3.0e38, op0=ALU.add, op1=ALU.min,
                                           accum_out=negmax[:, g:g + 1]).then_inc(S["negs_ready"], 1)

            def inverse(t, u, k):
                i = (t.part(u) + k) % 2
                for p in range(2):
                    dve.wait_ge(S["exp_done"], t.b(u, 4, 4 * k + 2 * p + 2))
                    V.reciprocal(rinv[i][:, 2 * p:2 * p + 2], psum_p[i][:, 2 * p:2 * p + 2]).then_inc(S["rinv_ready"], 1)

            def attn_residual(t):
                dve.wait_ge(S["wo_mm"], t.n(1, 0))
                dve.wait_ge(S["l_xtok"], t.n(16, 0))
                V.tensor_tensor(x1[:], gb[0][:], xtok_s[:], ALU.add).then_inc(S["x1_ready"], 1)

            def pick(t, z, ready, picks, rows_, bank, done):
                dve.wait_ge(S[ready], t.n(1, 0))
                n = t.n(2, -2)
                p = picks[0:rows_, n:n + 2] if isinstance(n, int) else picks[0:rows_, bass.ds(n, 2)]
                V.tensor_tensor(z[0:rows_, :].rearrange("p (u t) -> p u t", u=2),
                                ob[bank][0:rows_, 0:128].rearrange("p (u t) -> p u t", u=2),
                                p.unsqueeze(2).to_broadcast([rows_, 2, 64]), ALU.mult).then_inc(S[done], 1)

            def tile(t, first, last):
                keys_t(t, 0, 1)
                make_mask(t, 0, 1)
                if not first:
                    attn_residual(t)
                scores(t, 0, 1)
                inverse(t, 0, 1)

                def between():
                    if not first:
                        pick(t, z2m, "z2_mm", pick2, 64, 1, "z2_ready")
                    if not last:
                        make_mask(t, 1, 1)
                if last:
                    between()
                else:
                    query_tile(t, 1, between, gb[0])
                    keys_t(t, 1, 1)
                if not first:
                    pick(t, z3m, "z3_mm", pick3, 128, 1, "z3_ready")
                if not last:
                    scores(t, 1, 1)
                    inverse(t, 1, 1)

            t0 = Tile(0, 0)

            make_mask(t0, 0, 0)
            keys_t(t0, 0, 0)
            scores(t0, 0, 0)
            inverse(t0, 0, 0)
            tile(t0, True, False)
            with dve.Fori(0, TILES // 2 - 1) as j:
                for c in (1, 2):
                    tile(Tile(j, c), False, False)
            tile(Tile(TILES // 2 - 1, 1), False, True)
            end = Tile(TILES // 2, 0)
            attn_residual(end)
            pick(end, z2m, "z2_mm", pick2, 64, 1, "z2_ready")
            pick(end, z3m, "z3_mm", pick3, 128, 1, "z3_ready")

        @block.tensor
        def _(pe):
            mm = nc.tensor.matmul

            def dense(bank, lhs, rhs, more=None):
                for c in range(C):
                    last = mm(bank, lhs(c), rhs(c), start=(c == 0), stop=(c == C - 1 and more is None))
                return last

            def key_tile(r, rounds, free):
                i = r % 2
                pe.wait_ge(l_xt[r], rounds)
                after(pe, S["k_copied"], free)
                dense(gb[i][:], lambda c: xt_s[r][:, c, :], lambda c: wkv_s[:, c, :]).then_inc(S["ka_mm"], 1)

            def queries(loads, bank, xt_sb):
                pe.wait_ge(S["l_xq"], loads)
                dense(bank[:], lambda c: xt_sb[:, c, :], lambda c: wq_s[:, c, :]).then_inc(S["q_mm"], 1)

            def queries_t(n, bank):
                pe.wait_ge(S["q_rot"], n)
                o = bank[:].rearrange("p (a v q t) -> p a q v t", a=2, v=2, q=2)
                for k in range(4):
                    last = nc.tensor.transpose(o[:, k // 2, k % 2], qrot[:, 128 * k:128 * k + 128], ident)
                last.then_inc(S["qt_mm"], 1)

            pe.wait_ge(l_xt[0], 16)
            for c in range(C):
                pe.wait_ge(l_wkv[c], 16)
                last = mm(gb[0][:], xt_s[0][:, c, :], wkv_s[:, c, :], start=(c == 0), stop=(c == C - 1))
            last.then_inc(S["ka_mm"], 1)
            for n in range(1, 4):
                key_tile(n, 16, n - 1)
            HW = WS * NB // 2
            pe.wait_ge(S["blkd_ready"], 1)
            pe.wait_ge(S["l_few"], 16)
            bd = blkd[:].rearrange("p s b -> p (s b)")
            for i in range(2):
                last = mm(ob[i][0:NB, 0:HW], con("ones", NB), bd[:, HW * i:HW * i + HW], start=True, stop=True)
            last.then_inc(S["blkrow_mm"], 1)
            for n in range(4, HALF_A):
                key_tile(n - 4, 32, n - 1)
            pe.wait_ge(S["later_ready"], 1)
            pe.wait_ge(S["covered"], 1)
            for j in range(NW):
                for k in range(NW):
                    last = mm(tb[0][0:NB, BLOCK * j:BLOCK * j + BLOCK], later[:, k, NB * j:NB * j + NB],
                              cover[:, BLOCK * k:BLOCK * k + BLOCK], start=(k == 0), stop=(k == NW - 1))
            last.then_inc(S["lose_mm"], 1)
            pe.wait_ge(S["l_wq"], 16 * C)
            queries(16, sbk[0], ot_s)
            pe.wait_ge(S["wcode_ready"], 1)
            pe.wait_ge(S["blkrow_ev"], 2)
            for i in range(2):
                for j in range(NW):
                    last = mm(ob[i][0:BLOCK, 0:HW], wcode[:, BLOCK * j:BLOCK * j + BLOCK], same[:, j, HW * i:HW * i + HW],
                              start=(j == 0), stop=(j == NW - 1))
            last.then_inc(S["win_mm"], 1)
            pe.wait_ge(S["rows_ready"], 1)
            spread = con("spread", BLOCK).rearrange("p (s q) -> p s q", s=SP_)
            for k in range(2):
                src = rows[:, k, :].rearrange("p (c s b) -> p s c b", c=CH, s=SP_)
                for s in range(SP_):
                    last = mm(tb[0][0:KP, CH * NB * k:CH * NB * (k + 1)].rearrange("p (c b) -> p c b", c=CH),
                              spread[:, s, :], src[:, s], start=(s == 0), stop=(s == SP_ - 1))
            last.then_inc(S["idx_mm"], 1)

            with pe.Fori(HALF_A // 4, TILES // 4) as j:
                for r in range(4):
                    key_tile(r, j * 16 + 16, j * 4 + (r - 1))

            queries_t(1, sbk[1])
            pe.wait_ge(S["l_up"], 16 * (2 * C + 2))
            dense(tb[1][0:64, :], lambda c: a2_s[:, c, :], lambda c: wt_s[:, c, :]).then_inc(S["down_mm"], 1)
            dense(ob[0][0:64, :], lambda c: b2_s[:, c, :], lambda c: wpt_s[:, c, :]).then_inc(S["up_mm"], 1)
            pe.wait_ge(S["down_ev"], 1)
            for c in range(C):
                last = nc.tensor.transpose(ob[1][:, 64 * c:64 * c + 64], down_t[:, 128 * c:128 * c + 128], ident[0:64, 0:64])
            last.then_inc(S["downt_mm"], 1)

            def keys_t(t, u, k):
                r, done = t.ring(u + k)
                pe.wait_ge(kv_new[r], done)
                for p in range(2):
                    after(pe, S["pt_ev"], t.b(u, 4, 4 * (k - 2) + 3 + p))
                    for c in range(CH):
                        last = nc.tensor.transpose(tb[p][:, KP * c:KP * c + KP], kv_s[r][:, c, 128 * p:128 * p + 128],
                                                   ident[0:KP, 0:KP])
                    last.then_inc(S["kt_mm"], 1)

            def scores(t, u, k, heads):
                if (t.part(u) + k) % 2 == 0 and heads[0] == 0:
                    pe.wait_ge(S["qz_ready"], t.n(2, 2 * ((u + k) // 2) + 2))
                for g in heads:
                    p, h = g // 2, g % 2
                    pe.wait_ge(S["kt_ev"], t.b(u, 2, 2 * k + p + 1))
                    after(pe, S["negs_ready"], t.b(u, 4, 4 * k + g - 1))
                    v = (u + k) % 2
                    mm(sbk[g % 2][:, 0:WK], qz[:, h, 256 * p + 128 * v:256 * p + 128 * v + 128], kt_s[:, p, :],
                       start=True, stop=True).then_inc(S["s_mm"], 1)

            def probs_t(t, u, g, last_batch):
                i = t.part(u) % 2
                if g >= 2:
                    pe.wait_ge(S["pt_ev"], t.b(u, 4, g - 1))
                elif last_batch:
                    pe.wait_ge(S["pt_ev"], t.b(u, 4, g - 1))
                else:
                    pe.wait_ge(S["kt_ev"], t.b(u, 2, 2 + g + 1))
                pe.wait_ge(S["prob_ready"], t.b(u, 4, g + 1))
                for c in range(CH):
                    last = nc.tensor.transpose(tb[g % 2][0:KP, 128 * c:128 * c + 128], prob[i][:, g, KP * c:KP * c + KP], ident)
                last.then_inc(S["pt_mm"], 1)

            def values(t, u, p):
                r, _ = t.ring(u)
                pe.wait_ge(S["pt_ev"], t.b(u, 4, 2 * p + 2))
                after(pe, S["ot_ev"], t.b(u, 1, -1))
                for c in range(CH):
                    for h in range(2):
                        g = 2 * p + h
                        last = mm(ob[u][64 * h:64 * h + 64, 128 * p:128 * p + 128], kv_s[r][:, c, 256 + 64 * g:320 + 64 * g],
                                  pt_s[g][:, c, :], start=(c == 0), stop=(c == CH - 1))
                last.then_inc(S["pv_mm"], 1)

            def project(t):
                pe.wait_ge(S["ot_ev"], t.b(0, 1, 0))
                dense(gb[0][:], lambda c: ot_s[:, c, :], lambda c: wo_s[:, c, :]).then_inc(S["wo_mm"], 1)

            def layer1(t, queries_in_bank):
                pe.wait_ge(S["x1_ready"], t.n(1, 0))
                pe.wait_ge(S["w1i_ready"], t.n(1, 0))
                if queries_in_bank:
                    pe.wait_ge(S["qz_ready"], t.n(2, 2))
                for c in range(C):
                    last = mm(gb[1][:, 128 * c:128 * c + 128], x1[:, 128 * c:128 * c + 128], w1i[:], start=True, stop=True)
                last.then_inc(S["l1_mm"], 1)

            def ranks2(t):
                pe.wait_ge(S["x2_ready"], t.n(1, 0))
                dense(ob[1][0:64, 0:128], lambda c: down2[:, c, :], lambda c: x2t[:, c, :]).then_inc(S["z2_mm"], 1)

            def layer2(t):
                for k in range(C):
                    o = gb[1][:, 128 * k:128 * k + 128]
                    dense(o, lambda c: wb_s[:, c, 128 * k:128 * k + 128], lambda c: x2t[:, c, :], more=True)
                    if k == 0:
                        pe.wait_ge(S["z2_ready"], t.n(1, 0))
                    last = mm(o, up2[:, 128 * k:128 * k + 128], z2m[:], start=False, stop=True)
                last.then_inc(S["x3_mm"], 1)

            def ranks3(t):
                pe.wait_ge(S["x3_ready"], t.n(1, 0))
                dense(ob[1][:, 0:128], lambda c: a3_s[:, c, :], lambda c: x3t[:, c, :]).then_inc(S["z3_mm"], 1)

            def layer3(t, queries_in_bank):
                if queries_in_bank:
                    pe.wait_ge(S["q_t2"], t.n(1, 2))
                dense(gb[0][:], lambda c: x3t[:, c, :], lambda c: w3_s[:, c, :], more=True)
                pe.wait_ge(S["z3_ready"], t.n(1, 0))
                mm(gb[0][:], z3m[:], b3_s[:], start=False, stop=True).then_inc(S["out_mm"], 1)

            def tile(t, first, last):
                keys_t(t, 0, 1)
                if not first:
                    project(t)
                scores(t, 0, 1, (0, 1))
                probs_t(t, 0, 0, False)
                probs_t(t, 0, 1, False)
                scores(t, 0, 1, (2, 3))
                if not last:
                    if not first:
                        pe.wait_ge(S["x1_ready"], t.n(1, 0))
                    else:
                        pe.wait_ge(S["k_copied"], TILES)
                    queries(t.n(16, 32), gb[0], xt_s[0])
                if not first:
                    layer1(t, True)
                values(t, 0, 0)
                probs_t(t, 0, 2, False)
                probs_t(t, 0, 3, False)
                if not first:
                    ranks2(t)
                    layer2(t)
                values(t, 0, 1)
                if not last:
                    keys_t(t, 1, 1)
                if not first:
                    ranks3(t)
                if not last:
                    queries_t(t.n(1, 2), gb[1])
                if not first:
                    layer3(t, not last)
                probs_t(t, 1, 0, last)
                probs_t(t, 1, 1, last)
                if not last:
                    scores(t, 1, 1, (0, 1))
                values(t, 1, 0)
                probs_t(t, 1, 2, last)
                probs_t(t, 1, 3, last)
                if not last:
                    scores(t, 1, 1, (2, 3))
                values(t, 1, 1)

            pe.wait_ge(S["idx_ready"], 1)
            pe.wait_ge(S["downt_ev"], 1)
            pe.wait_ge(S["up_ev"], 1)
            pe.wait_ge(S["w_ident"], 1)
            pe.wait_ge(S["l_wo"], 16 * C)
            pe.wait_ge(S["l_low3"], 32)
            keys_t(Tile(0, 0), 0, 0)
            scores(Tile(0, 0), 0, 0, range(G))
            tile(Tile(0, 0), True, False)
            with pe.Fori(0, TILES // 2 - 1) as j:
                for c in (1, 2):
                    tile(Tile(j, c), False, False)
            tile(Tile(TILES // 2 - 1, 1), False, True)
            end = Tile(TILES // 2, 0)
            project(end)
            layer1(end, False)
            ranks2(end)
            layer2(end)
            ranks3(end)
            layer3(end, False)


def kernel(x, itok_Bx257_0_4111, itok_B_37_3939, itok_B_0_7, itok_B_0_3, itok_B_0_6,
           L0_cond_Wq, L0_cond_Wk, L0_cond_Wv, L0_cond_Wo, L0_cond_q_norm_scale, L0_cond_k_norm_scale,
           L0_cond_k_blocks, L0_cond_v_blocks, L1_cond_weights, L2_cond_W_base, L2_cond_Wt, L2_cond_A,
           L2_cond_B_w, L2_cond_Wp, L2_cond_scaling, L3_cond_W, L3_cond_A, L3_cond_Bm, L3_cond_scalings):
    import concourse.bacc as bacc
    from concourse.bass_utils import run_bass_kernel_spmd

    def chunks(a):
        a = np.asarray(a)
        return np.ascontiguousarray(a.reshape(-1, 128, a.shape[1]).transpose(1, 0, 2))

    x = np.asarray(x)
    xf = x.reshape(TILES, 128, D)
    wq = np.asarray(L0_cond_Wq).T.reshape(D, 2, 2, 2, HD)
    wo = np.asarray(L0_cond_Wo).T.reshape(2, 2, 2, HD, D)
    rows = np.concatenate([np.asarray(a).transpose(0, 2, 1, 3).reshape(NPOOL * BLOCK, G * HD)
                           for a in (L0_cond_k_blocks, L0_cond_v_blocks)], axis=1)
    arrays = dict(
        xt=np.ascontiguousarray(xf.reshape(TILES, 128, C, 128).transpose(0, 3, 2, 1)),
        xtok=np.ascontiguousarray(xf),
        kvrows=rows,
        wkv=chunks(np.concatenate([np.asarray(L0_cond_Wk), np.asarray(L0_cond_Wv)], axis=0).T),
        wq=chunks(wq.transpose(0, 1, 3, 2, 4).reshape(D, 512)),
        wo=chunks(wo.transpose(0, 2, 1, 3, 4).reshape(512, D)),
        qs=np.asarray(L0_cond_q_norm_scale), ks=np.asarray(L0_cond_k_norm_scale),
        w1=np.asarray(L1_cond_weights),
        wb=chunks(np.asarray(L2_cond_W_base).T),
        wt=chunks(L2_cond_Wt),
        a2t=chunks(np.asarray(L2_cond_A).reshape(NE2 * RANK, D).T),
        b2t=chunks(np.asarray(L2_cond_B_w).transpose(1, 0, 2).reshape(D, NE2 * RANK)),
        wpt=chunks(np.asarray(L2_cond_Wp).T),
        s2=np.repeat(np.asarray(L2_cond_scaling), RANK)[:, None],
        w3=chunks(np.asarray(L3_cond_W).T),
        a3t=chunks(np.asarray(L3_cond_A).reshape(NE3 * RANK, D).T),
        b3t=np.ascontiguousarray(np.asarray(L3_cond_Bm).transpose(0, 2, 1).reshape(NE3 * RANK, D)),
        s3=np.repeat(np.asarray(L3_cond_scalings), RANK)[:, None],
        table=np.lib.stride_tricks.sliding_window_view(
            np.concatenate([np.zeros(WS - NW, np.int32), np.asarray(itok_Bx257_0_4111).reshape(-1)]), WS), kvl=np.asarray(itok_B_37_3939),
        subj=np.asarray(itok_B_0_7).reshape(TILES, 1, 2),
        ad2=np.asarray(itok_B_0_3), ad3=np.asarray(itok_B_0_6),
        const=constants()[0], constf=constants()[1],
    )
    arrays = {n: np.ascontiguousarray(a) for n, a in arrays.items()}
    nc = bacc.Bacc("TRN2", target_bir_lowering=False, num_devices=1)
    args = {n: nc.dram_tensor(n + "_dram", a.shape, mybir.dt.from_np(a.dtype), kind="ExternalInput").ap()
            for n, a in arrays.items()}
    out = nc.dram_tensor("out_dram", (TILES, 128, D), mybir.dt.float32, kind="ExternalOutput").ap()
    build(nc, out=out, **args)
    r = run_bass_kernel_spmd(nc, [{n + "_dram": a for n, a in arrays.items()}], core_ids=[0])
    return r.results[0]["out_dram"].reshape(NB, NT, D)
```

```python
import concourse.bass as bass
from concourse import mybir
from contextlib import ExitStack
import numpy as np

NB, NT, D = 32, 64, 512
G, HD = 4, 64
BLOCK, WINDOW, NSLOT = 16, 256, 257
NPOOL = 16 * NSLOT
TILES = NB // 2
C = D // 128
WS = 21
NW = 5
WK = WS * BLOCK
CH = 3
KP = WK // CH
SP_ = KP // BLOCK
NE2, NE3, RANK = 4, 8, 16
STAGES = 3
NONE = 4096
NEG = 1.0e30

_WIDTHS = [[("ident", 128), ("diff", WK), ("negc", WK), ("inv", 32), ("tpos", 1), ("e2", 1), ("e3", 1),
            ("win", 1), ("toff", NW * BLOCK), ("code", 1)],
           [("order", NW * NW * NB), ("off", 1),
            ("spread", SP_ * KP), ("ones", NB)]]
CONST, NCONST = {}, [0, 0]
for _k in range(2):
    for _n, _w in _WIDTHS[_k]:
        CONST[_n] = (_k, NCONST[_k], _w)
        NCONST[_k] += _w


def constants():
    t = [np.zeros((rows, n), np.float32) for rows, n in zip((128, NB), NCONST)]

    def put(name, a):
        k, c, w = CONST[name]
        t[k][:a.shape[0], c:c + w] = a.reshape(a.shape[0], w)

    p = np.arange(128)
    put("ident", np.eye(128))
    put("diff", np.arange(WK)[None, :] - (p % NT)[:, None])
    put("negc", np.broadcast_to(-10000.0 * np.arange(WK), (128, WK)))
    inv = np.float32(1.0) / (np.float32(10000.0) ** (np.arange(32, dtype=np.float32) / np.float32(32)))
    put("inv", np.broadcast_to(inv.astype(np.float32), (128, 32)))
    put("tpos", (p % NT)[:, None])
    put("e2", (p // RANK)[:, None])
    put("e3", (p // RANK)[:, None])
    put("win", (NSLOT * np.arange(NB))[:, None])
    b = np.arange(NB)
    j = np.arange(NW)
    put("order", (NW * (b[:, None, None, None] - b[None, None, None, :]) + j[None, :, None, None] - j[None, None, :, None] > 0))
    put("toff", np.broadcast_to(np.arange(NW * BLOCK), (NB, NW * BLOCK)))
    put("code", (NT * b + 1)[:, None])
    put("off", np.arange(BLOCK)[:, None])
    q = np.arange(KP)
    put("spread", (q[None, None, :] == BLOCK * np.arange(SP_)[None, :, None] + np.arange(BLOCK)[:, None, None]))
    put("ones", np.ones((NB, NB)))
    return t


class Tile:

    def __init__(self, j, c):
        self.j, self.c = j, c

    def n(self, per, plus):
        return self.j * (2 * per) + (per * self.c + plus)

    def part(self, u):
        return 2 * self.c + u

    def b(self, u, per, plus):
        return self.j * (4 * per) + (per * self.part(u) + plus)

    def ring(self, u):
        q, r = divmod(self.part(u), 4)
        return r, self.j * 48 + 48 * (q + 1)


def after(eng, sem, value):
    if not isinstance(value, int) or value > 0:
        eng.wait_ge(sem, value)


def build(nc, xt, xtok, kvrows, wkv, wq, wo, qs, ks, w1, wb, wt, a2t, b2t, wpt, s2, w3, a3t, b3t, s3,
          table, kvl, subj, ad2, ad3, const, constf, out):
    f32, i32, f16, f32r = mybir.dt.float32, mybir.dt.int32, mybir.dt.float16, mybir.dt.float32r
    ALU, ACT, AX = mybir.AluOpType, mybir.ActivationFunctionType, mybir.AxisListType.X
    ctx = ExitStack()
    with ctx:
        def sb(name, shape, dt=f32):
            return ctx.enter_context(nc.sbuf_tensor(name, shape, dt))

        def sem(name):
            return ctx.enter_context(nc.semaphore(name))

        newkv = nc.dram_tensor("newkv", [NB * NT + 1, 2 * G * HD], f32).ap()
        newkv_t = newkv[1:NB * NT + 1, :].rearrange("(n p) f -> n p f", p=128)

        cst = [sb("cst", [128, NCONST[0]]), sb("cst_few", [NB, NCONST[1]])]

        def con(name, rows=128):
            k, c, w = CONST[name]
            return cst[k][0:rows, c:c + w]

        ident = con("ident")
        wb_s = sb("wb_s", [128, C, 512])
        wide = sb("wide", [128, 2, C, 512])
        wt_s, wpt_s = wide[:, 0], wide[:, 1]
        flat = wide[:].rearrange("p a c n -> p (a c n)")
        prob = [flat[:, G * WK * i:G * WK * (i + 1)].rearrange("p (g k) -> p g k", g=G) for i in range(2)]
        neg_s = flat[:, 2 * G * WK:3 * G * WK].rearrange("p (g k) -> p g k", g=G)
        windows = sb("windows", [128, 4 * CH * 512])
        kv_s = [windows[0:KP, CH * 512 * i:CH * 512 * (i + 1)].rearrange("p (c n) -> p c n", c=CH) for i in range(4)]
        same = windows[0:NB, 0:NW * WS * NB // 2].bitcast(f16).rearrange("p (j n) -> p j n", j=NW)
        rows = windows[0:BLOCK, NW * WS * NB:(NW + 2) * WS * NB].rearrange("p (k n) -> p k n", k=2)
        down2 = sb("down2", [128, C, 64])
        up2 = sb("up2", [128, 512])
        scl2, scl3 = sb("scl2", [128, 1]), sb("scl3", [128, 1])
        idx2, idx3 = sb("idx2", [128, NB], i32), sb("idx3", [128, NB], i32)
        pick2, pick3 = sb("pick2", [128, NB]), sb("pick3", [128, NB])
        kvb = sb("kvb", [128, NB], i32)
        kvi = sb("kvi", [128, NB], i32)
        k0f, r0f = sb("k0f", [128, NB]), sb("r0f", [128, NB])
        band = sb("band", [128, NB])
        limit = sb("limit", [128, NB])
        start = sb("start", [128, NB])
        pos = sb("pos", [128, TILES])
        nscale = {"q": sb("qscale", [128, 64]), "k": sb("kscale", [128, 64])}
        costab = {"q": sb("qcos", [128, TILES, 64])}
        sintab = {"q": sb("qsin", [128, TILES, 64])}
        kvc = sb("kvc", [NB, 2], i32)
        kvcf = sb("kvcf", [NB, 3])
        first_slot = sb("first_slot", [NB, 1], i32)
        blk_i = sb("blk_i", [NB, WS], i32)
        blk = sb("blk", [NB, WS])
        cover = sb("cover", [NB, NW * BLOCK], f16)
        code = sb("code", [NB, NW * BLOCK])
        wcode = sb("wcode", [NB, NW * BLOCK], f16)
        idx_all = sb("idx_all", [KP, NB, 2 * CH], i32)
        idx_b = [sb(f"idx_b{i}", [KP, 2 * CH], i32) for i in range(2)]
        xt_s = [sb("xt_s0", [128, C, 128])]
        nr = {}
        for w, h in (("q", 8), ("k", 4)):
            nr[w] = dict(sq=sb(w + "_sq", [128, h, 64]), ss=sb(w + "_ss", [128, h]), ms=sb(w + "_ms", [128, h]),
                         rstd=sb(w + "_rstd", [128, h]), t1=sb(w + "_t1", [128, h, 64]),
                         t2=sb(w + "_t2", [128, h, 64]))
        half = sb("half", [128, 8])
        qrot = sb("qrot", [128, 512])
        q_lo = [sb(f"q_lo{h}", [128, 512], f32r) for h in range(2)]
        negmax = sb("negmax", [128, G])
        psum_p = [sb(f"psum_p{i}", [128, G]) for i in range(2)]
        rinv = [sb(f"rinv{i}", [128, G]) for i in range(2)]
        w1raw = sb("w1raw", [128, 128])
        z2m = sb("z2m", [128, 128])
        subj_s = sb("subj_s", [1, 2], i32)

        w3_s = [sb(f"w3_{w}", [128, C, 512], f32r) for w in ("hi", "lo")]
        wq_s = [sb(f"wq_{w}", [128, C, 512], f32r) for w in ("hi", "lo")]
        xq_s = [sb(f"xq_{w}", [128, C, 128], f32r) for w in ("hi", "lo")]
        wo_s = [sb(f"wo_{w}", [128, C, 512], f32r) for w in ("hi", "lo")]

        early_ctx = ctx.enter_context(ExitStack())

        def early(name, shape, dt=f32):
            return early_ctx.enter_context(nc.sbuf_tensor(name, shape, dt))

        ang = early("ang", [128, TILES, 32])
        turns = early("turns", [128, TILES, 32])
        rest = early("rest", [128, TILES, 32])
        sinx = early("sinx", [128, TILES, 32])
        nsinx = early("nsinx", [128, TILES, 32])
        cosx = early("cosx", [128, TILES, 32])
        blkd = early("blkd", [NB, WS, NB])
        blkrow = early("blkrow", [NB, WS, NB])
        later = early("later", [NB, NW, NW * NB], f16)
        wt_tok = early("wt_tok", [NB, NW * BLOCK])
        wt_ge = early("wt_ge", [NB, NW * BLOCK])
        none = early("none", [BLOCK, WS * NB])
        down_t = early("down_t", [64, 512])
        wkv_s = early("wkv_s", [128, C, 512])
        a2_s = early("a2_s", [128, C, 64])
        b2_s = early("b2_s", [128, C, 64])
        kvo = [early(f"kvo{i}", [128, 512]) for i in range(2)]
        costab["k"], sintab["k"] = early("kcos", [128, TILES, 64]), early("ksin", [128, TILES, 64])
        xq_first = early("xq_first", [128, C, 128])
        xt_s += [early(f"xt_s{i}", [128, C, 128]) for i in range(1, 4)]
        stage = [early(f"stage{i}", [128, 512]) for i in range(STAGES)]
        early_ctx.close()

        xtok_s = sb("xtok_s", [128, 512])
        a3_s = sb("a3_s", [128, C, 128])
        b3_s = sb("b3_s", [128, 512])
        q_hi = [sb(f"q_hi{h}", [128, 512], f32r) for h in range(2)]
        kt_s = [sb(f"kt_s{g}", [128, WK], f32r) for g in range(G)]
        mask = [sb(f"mask{i}", [128, WK]) for i in range(2)]
        pt_s = [sb(f"pt_s{i}", [KP, CH, 128]) for i in range(G)]
        x1 = sb("x1", [128, 512])
        w1i = sb("w1i", [128, 128])
        x2t = sb("x2t", [128, C, 128])
        x3t = sb("x3t", [128, C, 128])
        x3s = [sb(f"x3_{w}", [128, C, 128], f32r) for w in ("hi", "lo")]
        ot_s = [sb(f"ot_{w}", [128, 4, 128], f32r) for w in ("hi", "lo")]
        z3m = sb("z3m", [128, 128])
        xo = sb("xo", [128, 512])

        gb = [ctx.enter_context(nc.psum_tensor(f"gb{i}", [128, 512], f32)) for i in range(2)]
        sbk = [ctx.enter_context(nc.psum_tensor(f"sbk{i}", [128, 512], f32)) for i in range(2)]
        tb = [ctx.enter_context(nc.psum_tensor(f"tb{i}", [128, 512], f32)) for i in range(2)]
        ob = [ctx.enter_context(nc.psum_tensor(f"ob{i}", [128, 512], f32)) for i in range(2)]

        names = """row0_stored l_const l_few l_table l_kvc l_kv l_scale l_wb l_low3 l_up l_ad
            set_dve blk_ready zeroed tab_ready sin_done slot_ready scale_ready qtab_ready
            blkd_ready blkrow_mm blkrow_ev covered same_ready rows0_ready later_ready lose_mm wcode_ready win_mm rows_ready
            idx_mm idx_ready down_mm down_ev downt_mm downt_ev up_mm up_ev w_ident diag_added split_hi split_lo
            ka_mm k_sq k_copied k_ss k_ms k_rstd k_t2 k_n k_rot
            q_mm q_sq q_ss q_ms q_rstd q_n q_t2 q_rot qt_mm qhi_ready qlo_ready l_xq xq_hi xq_lo
            kt_mm kt_hi kt_ev s_mm mask_band mask_start mask_ready negs_ready exp_done rinv_ready prob_ready
            pt_mm pt_ev pv_mm ot_hi ot_lo idx_copied
            wo_mm x1_ready l_xtok l_subj l_w1 w1i_ready l1_mm x2_ready z2_mm z2_ready x3_mm x3_ready x3_hi x3_lo
            z3_mm z3_ready out_mm xo_ready stored""".split()
        S = {n: sem(n) for n in names}
        l_wkv = [sem(f"l_wkv{i}") for i in range(C)]
        l_stage = [sem(f"l_stage{i}") for i in range(STAGES)]
        l_xt = [sem(f"l_xt{i}") for i in range(4)]
        kv_stored = [sem(f"kv_stored{i}") for i in range(2)]
        kv_old = [sem(f"kv_old{i}") for i in range(4)]
        kv_new = [sem(f"kv_new{i}") for i in range(4)]
        block = ctx.enter_context(nc.Block())

        def wait_alone(eng, *waits):
            waits = [(sem, v if isinstance(v, int) else eng.snap(eng.to_reg(v)))
                     for sem, v in waits if not isinstance(v, int) or v > 0]
            if waits:
                eng.wait_ge(S["l_const"], 16)
                for sem, v in waits:
                    eng.wait_ge(sem, v)

        splits = [(w[0][:, c], w[1][:, c], src[:, c], c if w is w3_s else None) for w, src in ((wq_s, wq), (w3_s, w3), (wo_s, wo)) for c in range(C)]
        HALF_A = TILES // 2

        def tables(eng, w):
            lo, hi = (nscale[w][:, 32 * a:32 * a + 32].unsqueeze(1).to_broadcast([128, TILES, 32]) for a in (0, 1))
            return [eng.tensor_tensor(costab[w][:, :, 0:32], cosx[:], lo, ALU.mult),
                    eng.tensor_tensor(costab[w][:, :, 32:64], cosx[:], hi, ALU.mult),
                    eng.tensor_tensor(sintab[w][:, :, 32:64], sinx[:], lo, ALU.mult),
                    eng.tensor_tensor(sintab[w][:, :, 0:32], nsinx[:], hi, ALU.mult)]

        @block.sync
        def _(sp):
            def load_xt(n, i):
                sp.dma_start(xt_s[i][:], xt[n]).then_inc(l_xt[i], 16)

            load_xt(0, 0)
            for c in range(C):
                sp.dma_start(wkv_s[:, c], wkv[:, c]).then_inc(l_wkv[c], 16)
            for i in range(1, 4):
                load_xt(i, i)
            for w, src in (("q", qs), ("k", ks)):
                sp.dma_start(nscale[w][:], src.partition_broadcast(128)).then_inc(S["l_scale"], 16)

            def store_kv(n, i):
                sp.wait_ge(S["k_rot"], n + 1)
                sp.dma_start(newkv_t[n], kvo[i][:]).then_inc(kv_stored[i], 16)

            pieces = [(w[:, c], src[:, c], name) for w, src, name in
                      ((wb_s, wb, "l_wb"), (wt_s, wt, "l_up"), (wpt_s, wpt, "l_up")) for c in range(C)]
            pieces += [(a2_s[:], a2t, "l_up"), (b2_s[:], b2t, "l_up")]
            each = -(-len(pieces) // (TILES - 4))
            for n in range(TILES):
                if n < TILES - 4:
                    sp.wait_ge(S["ka_mm"], n + 1)
                    load_xt(n + 4, n % 4)
                store_kv(n, n % 2)
                if n == 0:
                    sp.dma_start(xq_first[:], xt[0]).then_inc(S["l_xq"], 16)
                i = n if n < STAGES else n - 2 if n - 2 >= STAGES else len(splits)
                if i < len(splits):
                    if i >= STAGES:
                        sp.wait_ge(S["split_lo"], i - STAGES + 1)
                    sp.dma_start(stage[i % STAGES][:], splits[i][2]).then_inc(l_stage[i % STAGES], 16)
                for dst, src, name in pieces[n * each:(n + 1) * each]:
                    sp.dma_start(dst, src).then_inc(S[name], 16)

            def load_xq(n, before):
                after(sp, S["xq_lo"], before)
                sp.dma_start(xt_s[0][:], xt[n]).then_inc(S["l_xq"], 16)

            def tile(t, first, last):
                if not last:
                    load_xq(t.n(1, 1), 0 if first else t.n(1, 1))
                after(sp, S["x1_ready"], t.n(1, 0))
                sp.dma_start(xtok_s[:], xtok[t.n(1, 0)]).then_inc(S["l_xtok"], 16)
                sp.dma_start(subj_s[:], subj[t.n(1, 0)]).then_inc(S["l_subj"], 16)
                after(sp, S["w1i_ready"], t.n(1, 0))
                wait_alone(sp, (S["l_subj"], t.n(16, 16)))
                for u in range(2):
                    s = sp.value_load(subj_s[0:1, u:u + 1], min_val=0, max_val=7)
                    sp.dma_start(w1raw[64 * u:64 * u + 64, 64 * u:64 * u + 64], w1[s]).then_inc(S["l_w1"], 16)
                if not first:
                    sp.wait_ge(S["xo_ready"], t.n(1, 0))
                    sp.dma_start(out[t.n(1, -1)], xo[:]).then_inc(S["stored"], 16)

            sp.wait_ge(S["ka_mm"], TILES)
            sp.dma_start(a3_s[:], a3t).then_inc(S["l_low3"], 16)
            sp.dma_start(b3_s[:], b3t).then_inc(S["l_low3"], 16)
            sp.wait_ge(S["zeroed"], 1)
            tile(Tile(0, 0), True, False)
            with sp.Fori(0, TILES // 2 - 1) as j:
                for c in (1, 2):
                    tile(Tile(j, c), False, False)
            tile(Tile(TILES // 2 - 1, 1), False, True)
            sp.wait_ge(S["xo_ready"], TILES)
            sp.dma_start(out[TILES - 1], xo[:]).then_inc(S["stored"], 16)
            sp.wait_ge(S["stored"], 16 * (TILES + 1))

        @block.gpsimd
        def _(pool):
            nc.gpsimd.dma_start(kvc[:, 0:1], kvl.rearrange("(b a) -> b a", a=1)).then_inc(S["l_kvc"], 16)
            nc.gpsimd.memset(half[:], -0.5)
            for h in range(2):
                nc.gpsimd.memset(q_lo[h][:].bitcast(f32), 0.0)
            nc.gpsimd.memset(up2[:], 0.0)
            nc.gpsimd.memset(z2m[:], 0.0)
            nc.gpsimd.memset(w1raw[:], 0.0).then_inc(S["zeroed"], 1)
            pool.wait_ge(S["zeroed"], 1)
            nc.gpsimd.dma_start(newkv[0:1, :], up2[127:128, :]).then_inc(S["row0_stored"], 16)

            def root(w, h, value):
                pool.wait_ge(S[w + "_ms"], value)
                nc.gpsimd.tensor_tensor(nr[w]["rstd"][:], nr[w]["ms"][:], half[:, 0:h], ALU.pow).then_inc(S[w + "_rstd"], 1)

            P = nc.gpsimd
            pool.wait_ge(S["slot_ready"], 1)
            P.indirect_dma_start(blk_i[:], None, table, bass.IndirectOffsetOnAxis(ap=first_slot[:], axis=0),
                                 bounds_check=NB * NSLOT - WS, oob_is_err=False).then_inc(S["l_table"], 16)
            pool.wait_ge(S["l_table"], 16)
            P.tensor_copy(blk[:], blk_i[:]).then_inc(S["blk_ready"], 1)
            pool.wait_ge(S["blk_ready"], 1)
            pool.wait_ge(S["l_const"], 16)
            P.tensor_tensor(blkd[:], blk[:].unsqueeze(2).to_broadcast([NB, WS, NB]),
                            con("ident", NB)[:, 0:NB].unsqueeze(1).to_broadcast([NB, WS, NB]), ALU.mult).then_inc(S["blkd_ready"], 1)
            for n in range(4):
                root("k", 4, n + 1)
            pool.wait_ge(S["scale_ready"], 1)
            pool.wait_ge(S["sin_done"], 1)
            def add_identity(i):
                raw, c = stage[i % STAGES], splits[i][3]
                if c is not None:
                    pool.wait_ge(l_stage[i % STAGES], 16 * (i // STAGES + 1))
                    d = raw[:, 128 * c:128 * c + 128]
                    P.tensor_tensor(d, d, ident, ALU.add).then_inc(S["diag_added"], 1)

            def split_low(i):
                hi, lo, _, _ = splits[i]
                pool.wait_ge(S["split_hi"], i + 1)
                P.tensor_tensor(lo, stage[i % STAGES][:], hi.bitcast(f32), ALU.subtract).then_inc(S["split_lo"], 1)

            pool.wait_ge(S["blkrow_ev"], 2)
            brow = blkrow[:].rearrange("p s b -> p (s b)")
            for j in range(NW - 2, NW):
                last = P.tensor_scalar(same[:, j, :], brow, blk[:, WS - NW + j:WS - NW + j + 1], None, ALU.is_equal)
            last.then_inc(S["same_ready"], 1)
            pool.wait_ge(S["l_few"], 16)
            P.tensor_scalar(rows[:, 0, :], brow[0:BLOCK], float(BLOCK), con("off", BLOCK), ALU.mult,
                            ALU.add).then_inc(S["rows0_ready"], 1)
            pool.wait_ge(S["xq_hi"], 1)
            P.tensor_tensor(xq_s[1][:], xq_first[:], xq_s[0][:].bitcast(f32), ALU.subtract).then_inc(S["xq_lo"], 1)
            for n in range(4, HALF_A):
                root("k", 4, n + 1)
                split_low(n - 4)
            tables(P, "q")[-1].then_inc(S["qtab_ready"], 1)
            for c in range(C):
                if c == 0:
                    pool.wait_ge(S["l_wb"], 16 * C)
                d = wb_s[:, c, 128 * c:128 * c + 128]
                last = nc.gpsimd.tensor_tensor(d, d, ident, ALU.add)
            last.then_inc(S["w_ident"], 1)
            root("q", 8, 1)

            def copy_index(t, u, k):
                i = (t.part(u) + k) % 2
                n = t.b(u, 1, k)
                src = idx_all[:, n:n + 1, :] if isinstance(n, int) else idx_all[:, bass.ds(n, 1), :]
                nc.gpsimd.tensor_copy(idx_b[i][:], src.rearrange("p a k -> p (a k)")).then_inc(S["idx_copied"], 1)

            def gather(t, u, k, new):
                r, done = t.ring(u + k)
                i = (t.part(u) + k) % 2
                for c in range(CH):
                    nc.gpsimd.indirect_dma_start(
                        kv_s[r][:, c, :], None, newkv if new else kvrows,
                        bass.IndirectOffsetOnAxis(ap=idx_b[i][:, new * CH + c:new * CH + c + 1], axis=0),
                        bounds_check=NB * NT if new else NPOOL * BLOCK - 1, oob_is_err=False,
                    ).then_inc((kv_new if new else kv_old)[r], 16)

            t0 = Tile(0, 0)

            def gather_first(k):
                copy_index(t0, 0, k)
                pool.wait_ge(S["idx_copied"], k + 1)
                gather(t0, 0, k, 0)

            add_identity(C)
            pool.wait_ge(S["idx_ready"], 1)
            gather_first(0)
            for n in range(HALF_A, TILES):
                root("k", 4, n + 1)
                split_low(n - 4)
                if n + 1 < TILES:
                    add_identity(n - 3)

            def lay_over(t, u, k):
                r, done = t.ring(u + k)
                wait_alone(pool, (kv_old[r], done))
                gather(t, u, k, 1)

            def norm(t, u, k):
                i = (t.part(u) + k) % 2
                for g in range(G):
                    wait_alone(pool, (S["rinv_ready"], t.b(u, 2, 2 * k + g // 2 + 1)))
                    nc.gpsimd.tensor_scalar(prob[i][:, g, :], prob[i][:, g, :], rinv[i][:, g:g + 1], 1.0,
                                            ALU.mult, ALU.mult).then_inc(S["prob_ready"], 1)

            def w1_ident(t):
                pool.wait_ge(S["l_w1"], t.n(32, 32))
                after(pool, S["l1_mm"], t.n(1, 0))
                nc.gpsimd.tensor_tensor(w1i[:], w1raw[:], ident, ALU.add).then_inc(S["w1i_ready"], 1)

            def slot(t, u, b_left):
                if u == 1 and b_left > 0:
                    root("q", 8, t.n(1, 2))
                if b_left >= 3:
                    r, done = t.ring(u + 1)
                    pool.wait_ge(kv_new[r], done)
                    copy_index(t, u, 3)
                    wait_alone(pool, (S["idx_copied"], t.b(u, 1, 4)), (S["pv_mm"], t.b(u, 2, 0)))
                    gather(t, u, 3, 0)
                if b_left >= 2:
                    lay_over(t, u, 2)
                if u == 1:
                    w1_ident(t)
                if b_left >= 1:
                    norm(t, u, 1)

            gather_first(1)
            pool.wait_ge(S["row0_stored"], 16)
            for i in range(2):
                pool.wait_ge(kv_stored[i], 16 * TILES // 2)
            for k in range(2):
                lay_over(t0, 0, k)
            r, done = t0.ring(0)
            pool.wait_ge(kv_new[r], done)
            copy_index(t0, 0, 2)
            pool.wait_ge(S["idx_copied"], 3)
            gather(t0, 0, 2, 0)
            norm(t0, 0, 0)
            slot(t0, 0, NB - 1)
            slot(t0, 1, NB - 2)
            with pool.Fori(0, TILES // 2 - 2) as j:
                for c in (1, 2):
                    for u in range(2):
                        slot(Tile(j, c), u, 3)
            for c in (1, 2, 3):
                for u in range(2):
                    slot(Tile(TILES // 2 - 2, c), u, 2 * (3 - c) + 1 - u)

        @block.scalar
        def _(act):
            act.dma_start(kvb[:], kvl.partition_broadcast(128)).then_inc(S["l_kv"], 16)
            act.dma_start(cst[0][:], const).then_inc(S["l_const"], 16)
            act.dma_start(cst[1][:], constf).then_inc(S["l_few"], 16)
            for d, s in ((scl2[0:64], s2), (scl3[:], s3), (idx2[:], ad2.partition_broadcast(128)),
                         (idx3[:], ad3.partition_broadcast(128))):
                act.dma_start(d, s).then_inc(S["l_ad"], 16)
            act.wait_ge(S["tab_ready"], 1)
            nc.scalar.activation(sinx[:], rest[:], ACT.Sin)
            nc.scalar.activation(nsinx[:], rest[:], ACT.Sin, scale=-1.0)
            nc.scalar.activation(cosx[:], turns[:], ACT.Sin).then_inc(S["sin_done"], 1)

            def key_tile(n, i, free):
                act.wait_ge(S["ka_mm"], n + 1)
                after(act, S["k_ss"], n)
                nc.scalar.activation(nr["k"]["sq"][:], gb[i][:, 0:256].rearrange("p (g d) -> p g d", g=G),
                                     ACT.Square).then_inc(S["k_sq"], 1)
                after(act, kv_stored[i], free)
                nc.scalar.activation(kvo[i][:], gb[i][:], ACT.Copy).then_inc(S["k_copied"], 1)

            def square(n, bank):
                act.wait_ge(S["q_mm"], n)
                nc.scalar.activation(nr["q"]["sq"][:], bank[:].rearrange("p (h d) -> p h d", h=8),
                                     ACT.Square).then_inc(S["q_sq"], 1)

            def queries(n, used, bank):
                act.wait_ge(S["qt_mm"], n)
                after(act, S["s_mm"], used)
                for h in range(2):
                    for side in range(2):
                        nc.scalar.activation(q_hi[h][64 * side:64 * side + 64, :], bank[64 * h:64 * h + 64, :],
                                             ACT.Copy).then_inc(S["qhi_ready"], 1)

            for n in range(4):
                key_tile(n, n % 2, 16 * (n // 2))
            HW = WS * NB // 2

            def evac(dst, src, ready, done):
                act.wait_ge(S[ready], 1)
                nc.scalar.activation(dst, src, ACT.Copy).then_inc(S[done], 1)
            brow = blkrow[:].rearrange("p s b -> p (s b)")
            for i in range(2):
                evac(brow[:, HW * i:HW * i + HW], ob[i][0:NB, 0:HW], "blkrow_mm", "blkrow_ev")
            def split_high(i):
                act.wait_ge(l_stage[i % STAGES], 16 * (i // STAGES + 1))
                after(act, S["diag_added"], min(i + 1 - C, C))
                nc.scalar.activation(splits[i][0], stage[i % STAGES][:], ACT.Copy).then_inc(S["split_hi"], 1)

            def xq_high(count, src, ready):
                act.wait_ge(S["l_xq"], 16 * count if isinstance(count, int) else ready)
                after(act, S["q_mm"], count - 1)
                nc.scalar.activation(xq_s[0][:], src[:], ACT.Copy).then_inc(S["xq_hi"], 1)

            xq_high(1, xq_first, 16)
            for n in range(4, HALF_A):
                key_tile(n, n % 2, 16 * (n // 2))
                split_high(n - 4)
            evac(idx_all[:], tb[0][0:KP, 0:2 * CH * NB].rearrange("p (k b) -> p b k", b=NB), "idx_mm", "idx_ready")
            square(1, sbk[0])
            for n in range(HALF_A, TILES):
                key_tile(n, n % 2, 16 * (n // 2))
                split_high(n - 4)
            act.wait_ge(S["zeroed"], 1)
            queries(1, 0, sbk[1])
            evac(down_t[:], tb[1][0:64, :], "down_mm", "down_ev")
            evac(up2[0:64, :], ob[0][0:64, :], "up_mm", "up_ev")
            evac(down2[:], ob[1][:, 0:C * 64].rearrange("p (c r) -> p c r", c=C), "downt_mm", "downt_ev")

            def keys_high(t, u, k):
                for g in range(G):
                    p, h = g // 2, g % 2
                    act.wait_ge(S["kt_mm"], t.b(u, 2, 2 * k + p + 1))
                    after(act, S["s_mm"], t.b(u, 4, 4 * (k - 1) + g + 1))
                    nc.scalar.activation(kt_s[g][64 * h:64 * h + 64, :], tb[p][64 * h:64 * h + 64, 0:WK],
                                         ACT.Copy).then_inc(S["kt_hi"], 1)

            def exps(t, u, k, g):
                i = (t.part(u) + k) % 2
                act.wait_ge(S["negs_ready"], t.b(u, 4, 4 * k + g + 1))
                after(act, S["pt_mm"], t.b(u, 4, 4 * (k - 2) + g + 1))
                nc.scalar.activation(prob[i][:, g, :], neg_s[:, g, :], ACT.Exp, bias=negmax[:, g:g + 1], scale=-1.0,
                                     accum_out=psum_p[i][:, g:g + 1]).then_inc(S["exp_done"], 1)

            def probs_t(t, u, g):
                act.wait_ge(S["pt_mm"], t.b(u, 4, g + 1))
                after(act, S["pv_mm"], t.b(u, 2, g // 2 - 1))
                nc.scalar.activation(pt_s[g][:], tb[g % 2][0:KP, 0:CH * 128].rearrange("p (c q) -> p c q", c=CH),
                                     ACT.Copy).then_inc(S["pt_ev"], 1)

            def attn_out(t, u):
                act.wait_ge(S["pv_mm"], t.b(u, 2, 2))
                after(act, S["wo_mm"], t.n(1, 0))
                nc.scalar.activation(ot_s[0][:, :, 64 * u:64 * u + 64],
                                     ob[u][:, 0:256].rearrange("p (k t) -> p k t", k=4), ACT.Copy).then_inc(S["ot_hi"], 1)

            def copy_bank(src, dst, ready, value, done):
                act.wait_ge(S[ready], value)
                nc.scalar.activation(dst, src, ACT.Copy).then_inc(S[done], 1)

            def layer1(t):
                copy_bank(gb[1][:].rearrange("p (c t) -> p c t", c=C), x2t[:], "l1_mm", t.n(1, 0), "x2_ready")

            def layer2(t):
                copy_bank(gb[1][:].rearrange("p (c t) -> p c t", c=C), x3t[:], "x3_mm", t.n(1, 0), "x3_ready")

            def layer2_high(t):
                copy_bank(x3t[:], x3s[0][:], "x3_ready", t.n(1, 0), "x3_hi")

            def layer3(t):
                act.wait_ge(S["out_mm"], t.n(1, 0))
                act.wait_ge(S["stored"], t.n(16, 0))
                nc.scalar.activation(xo[:], gb[0][:], ACT.Copy).then_inc(S["xo_ready"], 1)

            def tile(t, first, last):
                if not last:
                    xq_high(t.n(1, 2), xt_s[0], t.n(16, 32))
                keys_high(t, 0, 1)
                if not first:
                    exps(t, 0, 0, 2)
                    exps(t, 0, 0, 3)
                exps(t, 0, 1, 0)
                probs_t(t, 0, 0)
                exps(t, 0, 1, 1)
                probs_t(t, 0, 1)
                exps(t, 0, 1, 2)
                exps(t, 0, 1, 3)
                if not last:
                    square(t.n(1, 2), gb[0])
                if not first:
                    layer1(t)
                probs_t(t, 0, 2)
                probs_t(t, 0, 3)
                if not first:
                    layer2(t)
                if not first:
                    layer2_high(t)
                attn_out(t, 0)
                if not last:
                    keys_high(t, 1, 1)
                    queries(t.n(1, 2), t.b(1, 4, 4), gb[1])
                probs_t(t, 1, 0)
                probs_t(t, 1, 1)
                if not first:
                    layer3(t)
                probs_t(t, 1, 2)
                probs_t(t, 1, 3)
                if not last:
                    exps(t, 1, 1, 0)
                attn_out(t, 1)
                if not last:
                    exps(t, 1, 1, 1)

            act.sem_inc(S["stored"], 16)
            keys_high(Tile(0, 0), 0, 0)
            for g in range(G):
                exps(Tile(0, 0), 0, 0, g)
            tile(Tile(0, 0), True, False)
            with act.Fori(0, TILES // 2 - 1) as j:
                for c in (1, 2):
                    tile(Tile(j, c), False, False)
            tile(Tile(TILES // 2 - 1, 1), False, True)
            end = Tile(TILES // 2, 0)
            layer1(end)
            layer2(end)
            layer2_high(end)
            layer3(end)

        @block.vector
        def _(dve):
            n_set = [0]

            def link(ins):
                n_set[0] += 1
                ins.then_inc(S["set_dve"], 1)
                dve.wait_ge(S["set_dve"], n_set[0])

            V = nc.vector
            dve.wait_ge(S["l_kvc"], 16)
            link(V.tensor_scalar(kvc[:, 1:2], kvc[:, 0:1], 4, None, ALU.arith_shift_right))
            V.tensor_copy(kvcf[:, 1:2], kvc[:, 0:1])
            link(V.tensor_copy(kvcf[:, 0:1], kvc[:, 1:2]))
            dve.wait_ge(S["l_const"], 16)
            link(V.tensor_tensor(kvcf[:, 2:3], kvcf[:, 0:1], con("win", NB), ALU.add))
            V.tensor_copy(first_slot[:], kvcf[:, 2:3]).then_inc(S["slot_ready"], 1)
            link(V.scalar_tensor_tensor(kvcf[:, 1:2], kvcf[:, 0:1], -16.0, kvcf[:, 1:2], ALU.mult, ALU.add))
            link(V.tensor_scalar(wt_tok[:], con("toff", NB), kvcf[:, 1:2], None, ALU.subtract))
            link(V.tensor_scalar(wt_ge[:], wt_tok[:], 0.0, None, ALU.is_ge))
            link(V.scalar_tensor_tensor(cover[:], wt_tok[:], float(NT), wt_ge[:], ALU.is_lt, ALU.mult))
            V.scalar_tensor_tensor(code[:], wt_tok[:], con("code", NB), cover[:], ALU.add, ALU.mult).then_inc(S["covered"], 1)
            dve.wait_ge(S["l_kv"], 16)
            V.tensor_scalar(kvi[:], kvb[:], 4, None, ALU.arith_shift_right)
            V.tensor_copy(pos[0:64, :], kvb[0:64].rearrange("p (n u) -> p n u", u=2)[:, :, 0])
            link(V.tensor_copy(pos[64:128, :], kvb[64:128].rearrange("p (n u) -> p n u", u=2)[:, :, 1]))
            link(V.tensor_copy(k0f[:], kvi[:]))
            V.tensor_copy(r0f[:], kvb[:])
            link(V.tensor_scalar(pos[:], pos[:], con("tpos"), None, ALU.add))
            V.scalar_tensor_tensor(r0f[:], k0f[:], -16.0, r0f[:], ALU.mult, ALU.add)
            inv = con("inv").unsqueeze(1).to_broadcast([128, TILES, 32])
            link(V.tensor_tensor(ang[:], pos[:].unsqueeze(2).to_broadcast([128, TILES, 32]), inv, ALU.mult))
            MAGIC = 1.5 * 2.0 ** 23
            link(V.tensor_scalar(turns[:], ang[:], float(1.0 / (2.0 * np.pi)), MAGIC, ALU.mult, ALU.add))
            link(V.tensor_scalar(turns[:], turns[:], -MAGIC, None, ALU.add))
            c1 = 6.28125
            c2 = float(np.float32(np.round((2 * np.pi - c1) * 2.0 ** 22) / 2.0 ** 22))
            c3 = float(np.float32(2 * np.pi - c1 - c2))
            link(V.scalar_tensor_tensor(rest[:], turns[:], -c1, ang[:], ALU.mult, ALU.add))
            link(V.scalar_tensor_tensor(rest[:], turns[:], -c2, rest[:], ALU.mult, ALU.add))
            link(V.scalar_tensor_tensor(rest[:], turns[:], -c3, rest[:], ALU.mult, ALU.add))
            link(V.tensor_scalar(rest[:], rest[:], 3.1415925, -3.1415925, ALU.min, ALU.max))
            link(V.scalar_tensor_tensor(turns[:], rest[:], -1.0, rest[:], ALU.mult, ALU.max))
            V.tensor_scalar(turns[:], turns[:], -1.0, float(np.pi / 2), ALU.mult, ALU.add).then_inc(S["tab_ready"], 1)
            dve.wait_ge(S["l_scale"], 32)
            V.tensor_scalar(nscale["q"][:], nscale["q"][:], 1.0, None, ALU.add)
            V.tensor_scalar(nscale["k"][:], nscale["k"][:], 1.0, None, ALU.add).then_inc(S["scale_ready"], 1)
            dve.wait_ge(S["scale_ready"], 1)
            dve.wait_ge(S["sin_done"], 1)
            link(tables(V, "k")[-1])

            def norm_rotate(w, h, src, dst, tab, value, gate=None, between=None):
                def done(step):
                    return S[w + "_" + step]
                k = nr[w]
                dve.wait_ge(done("sq"), value)
                V.reduce_sum(k["ss"][:], k["sq"][:], AX).then_inc(done("ss"), 1)
                dve.wait_ge(done("ss"), value)
                V.tensor_scalar(k["ms"][:], k["ss"][:], 1.0 / HD, 1e-6, ALU.mult, ALU.add).then_inc(done("ms"), 1)
                cos, sin = (x[w][:, tab:tab + 1, :] if isinstance(tab, int) else x[w][:, bass.ds(tab, 1), :] for x in (costab, sintab))
                if w == "k":
                    dve.wait_ge(S["k_copied"], value)
                V.tensor_tensor(k["t1"][:], src, cos.to_broadcast([128, h, 64]), ALU.mult)
                V.tensor_tensor(k["t2"][:, :, 0:32], src[:, :, 32:64], sin[:, :, 0:32].to_broadcast([128, h, 32]), ALU.mult)
                V.tensor_tensor(k["t2"][:, :, 32:64], src[:, :, 0:32], sin[:, :, 32:64].to_broadcast([128, h, 32]),
                                ALU.mult).then_inc(done("t2"), 1)
                dve.wait_ge(done("t2"), value)
                V.tensor_tensor(k["t1"][:], k["t1"][:], k["t2"][:], ALU.add).then_inc(done("n"), 1)
                if between:
                    between()
                if gate:
                    gate()
                dve.wait_ge(done("rstd"), value)
                dve.wait_ge(done("n"), value)
                V.tensor_tensor(dst, k["t1"][:], k["rstd"][:].unsqueeze(2).to_broadcast([128, h, 64]),
                                ALU.mult).then_inc(done("rot"), 1)

            def key_tile(n, i):
                k = kvo[i][:, 0:256].rearrange("p (g d) -> p g d", g=G)
                norm_rotate("k", 4, k, k, n, n + 1)

            with dve.Fori(0, HALF_A // 4) as j:
                for i in range(2):
                    key_tile(j * 2 + i, i)
            dve.wait_ge(S["blkrow_ev"], 2)
            brow = blkrow[:].rearrange("p s b -> p (s b)")
            for j in range(NW - 2):
                last = V.tensor_scalar(same[:, j, :], brow, blk[:, WS - NW + j:WS - NW + j + 1], None, ALU.is_equal)
            link(last)
            dve.wait_ge(S["same_ready"], 1)
            dve.wait_ge(S["l_few"], 16)
            V.tensor_tensor(later[:], same[:, :, (WS - NW) * NB:], con("order", NB).rearrange("p (j e) -> p j e", j=NW),
                            ALU.mult).then_inc(S["later_ready"], 1)
            def split_xq(count, src):
                dve.wait_ge(S["xq_hi"], count)
                V.tensor_tensor(xq_s[1][:], src[:], xq_s[0][:].bitcast(f32), ALU.subtract).then_inc(S["xq_lo"], 1)

            with dve.Fori(HALF_A // 4, HALF_A // 2) as j:
                for i in range(2):
                    key_tile(j * 2 + i, i)
            dve.wait_ge(S["lose_mm"], 1)
            V.scalar_tensor_tensor(wcode[:], tb[0][0:NB, 0:NW * BLOCK], 0.0, code[:], ALU.is_equal, ALU.mult).then_inc(S["wcode_ready"], 1)
            HW = WS * NB // 2
            dve.wait_ge(S["win_mm"], 1)
            for i in range(2):
                w = ob[i][0:BLOCK, 0:HW]
                link(V.tensor_scalar(none[:, HW * i:HW * i + HW], w, 0.0, float(NONE), ALU.is_equal, ALU.mult))
                last = V.tensor_tensor(rows[:, 1, HW * i:HW * i + HW], w, none[:, HW * i:HW * i + HW], ALU.add)
            last.then_inc(S["rows_ready"], 1)

            V.tensor_scalar(band[:], r0f[:], 2.0, WINDOW + 1.0, ALU.mult, ALU.add)
            V.tensor_scalar(start[:], k0f[:], -160000.0, 2555000.0, ALU.mult, ALU.add)
            link(V.tensor_scalar(limit[:], r0f[:], -1.0, -WINDOW - 0.5, ALU.mult, ALU.add))
            V.scalar_tensor_tensor(limit[:], r0f[:], 0.5, limit[:], ALU.add, ALU.mult)
            dve.wait_ge(S["l_ad"], 64)
            V.tensor_scalar(pick2[0:64], idx2[0:64], con("e2", 64), scl2[0:64], ALU.is_equal, ALU.mult)
            V.tensor_scalar(pick3[:], idx3[:], con("e3"), scl3[:], ALU.is_equal, ALU.mult)
            def query_tile(t, plus, between, bank):
                norm_rotate("q", 8, bank[:].rearrange("p (h d) -> p h d", h=8), qrot[:].rearrange("p (h d) -> p h d", h=8),
                            t.n(1, plus), t.n(1, plus + 1), between=between,
                            gate=lambda: after(dve, S["qt_mm"], t.n(1, plus)))

            dve.wait_ge(S["qtab_ready"], 1)
            query_tile(Tile(0, 0), 0, None, sbk[0])

            with dve.Fori(HALF_A // 2, TILES // 2) as j:
                for i in range(2):
                    key_tile(j * 2 + i, i)

            dve.wait_ge(S["zeroed"], 1)

            def make_mask(t, u, k):
                m = mask[(t.part(u) + k) % 2]
                n = t.b(u, 1, k)
                col = (lambda a: a[:, n:n + 1]) if isinstance(n, int) else (lambda a: a[:, bass.ds(n, 1)])
                V.scalar_tensor_tensor(m[:], con("diff"), col(band), con("diff"), ALU.subtract, ALU.mult).then_inc(S["mask_band"], 1)
                dve.wait_ge(S["mask_band"], t.b(u, 1, k + 1))
                V.scalar_tensor_tensor(m[:], con("negc"), col(start), m[:], ALU.add, ALU.max).then_inc(S["mask_start"], 1)
                dve.wait_ge(S["mask_start"], t.b(u, 1, k + 1))
                V.tensor_scalar(m[:], m[:], col(limit), -NEG, ALU.is_gt, ALU.mult).then_inc(S["mask_ready"], 1)

            def keys_t(t, u, k):
                for g in range(G):
                    p, h = g // 2, g % 2
                    dve.wait_ge(S["kt_hi"], t.b(u, 4, 4 * k + g + 1))
                    V.tensor_tensor(kt_s[g][64 * (1 - h):64 * (1 - h) + 64, :], tb[p][64 * h:64 * h + 64, 0:WK],
                                    kt_s[g][64 * h:64 * h + 64, :].bitcast(f32), ALU.subtract).then_inc(S["kt_ev"], 1)

            def queries_low(n, bank):
                for h in range(2):
                    dve.wait_ge(S["qhi_ready"], n * 4 + (2 * h - 2))
                    V.tensor_tensor(q_lo[h][64 * h:64 * h + 64, :], bank[64 * h:64 * h + 64, :],
                                    q_hi[h][64 * h:64 * h + 64, :].bitcast(f32), ALU.subtract).then_inc(S["qlo_ready"], 1)

            def scores(t, u, k, heads=range(G)):
                dve.wait_ge(S["mask_ready"], t.b(u, 1, k + 1))
                for g in heads:
                    wait_alone(dve, (S["s_mm"], t.b(u, 4, 4 * k + g + 1)),
                               (S["exp_done"], t.b(u, 4, 4 * (k - 1) + g + 1)))
                    V.tensor_tensor_reduce(out=neg_s[:, g, :], in0=sbk[g % 2][:, 0:WK], in1=mask[(t.part(u) + k) % 2][:],
                                           scale=-1.0 / 16, scalar=3.0e38, op0=ALU.add, op1=ALU.min,
                                           accum_out=negmax[:, g:g + 1]).then_inc(S["negs_ready"], 1)

            def inverse(t, u, k, p):
                i = (t.part(u) + k) % 2
                dve.wait_ge(S["exp_done"], t.b(u, 4, 4 * k + 2 * p + 2))
                V.reciprocal(rinv[i][:, 2 * p:2 * p + 2], psum_p[i][:, 2 * p:2 * p + 2]).then_inc(S["rinv_ready"], 1)

            def attn_residual(t):
                dve.wait_ge(S["wo_mm"], t.n(1, 0))
                dve.wait_ge(S["l_xtok"], t.n(16, 0))
                V.tensor_tensor(x1[:], gb[0][:], xtok_s[:], ALU.add).then_inc(S["x1_ready"], 1)

            def split_x3(t):
                dve.wait_ge(S["x3_hi"], t.n(1, 0))
                V.tensor_tensor(x3s[1][:], x3t[:], x3s[0][:].bitcast(f32), ALU.subtract).then_inc(S["x3_lo"], 1)

            def split_attn(t, u):
                dve.wait_ge(S["ot_hi"], t.b(u, 1, 1))
                V.tensor_tensor(ot_s[1][:, :, 64 * u:64 * u + 64], ob[u][:, 0:256].rearrange("p (k t) -> p k t", k=4),
                                ot_s[0][:, :, 64 * u:64 * u + 64].bitcast(f32), ALU.subtract).then_inc(S["ot_lo"], 1)

            def pick(t, z, ready, picks, rows_, bank, done):
                dve.wait_ge(S[ready], t.n(1, 0))
                n = t.n(2, -2)
                p = picks[0:rows_, n:n + 2] if isinstance(n, int) else picks[0:rows_, bass.ds(n, 2)]
                V.tensor_tensor(z[0:rows_, :].rearrange("p (u t) -> p u t", u=2),
                                ob[bank][0:rows_, 0:128].rearrange("p (u t) -> p u t", u=2),
                                p.unsqueeze(2).to_broadcast([rows_, 2, 64]), ALU.mult).then_inc(S[done], 1)

            def tile(t, first, last):
                if not last:
                    split_xq(t.n(1, 2), xt_s[0])
                keys_t(t, 0, 1)
                scores(t, 0, 1, (0, 1))
                if not first:
                    attn_residual(t)
                    inverse(t, 0, 0, 1)
                scores(t, 0, 1, (2, 3))
                inverse(t, 0, 1, 0)
                inverse(t, 0, 1, 1)

                def between():
                    if not first:
                        pick(t, z2m, "z2_mm", pick2, 64, 1, "z2_ready")
                    if not last:
                        make_mask(t, 1, 1)
                        make_mask(t, 1, 2)
                if last:
                    between()
                else:
                    query_tile(t, 1, between, gb[0])
                if not first:
                    split_x3(t)
                    pick(t, z3m, "z3_mm", pick3, 128, 1, "z3_ready")
                if not last:
                    keys_t(t, 1, 1)
                split_attn(t, 0)
                if not last:
                    queries_low(t.n(1, 2), gb[1])
                    scores(t, 1, 1, (0, 1))
                split_attn(t, 1)
                if not last:
                    scores(t, 1, 1, (2, 3))
                    inverse(t, 1, 1, 0)

            t0 = Tile(0, 0)

            queries_low(1, sbk[1])
            make_mask(t0, 0, 0)
            make_mask(t0, 0, 1)
            keys_t(t0, 0, 0)
            scores(t0, 0, 0)
            inverse(t0, 0, 0, 0)
            inverse(t0, 0, 0, 1)
            tile(t0, True, False)
            with dve.Fori(0, TILES // 2 - 1) as j:
                for c in (1, 2):
                    tile(Tile(j, c), False, False)
            tile(Tile(TILES // 2 - 1, 1), False, True)
            end = Tile(TILES // 2, 0)
            attn_residual(end)
            pick(end, z2m, "z2_mm", pick2, 64, 1, "z2_ready")
            split_x3(end)
            pick(end, z3m, "z3_mm", pick3, 128, 1, "z3_ready")

        @block.tensor
        def _(pe):
            mm = nc.tensor.matmul

            def dense(bank, lhs, rhs, more=None):
                for c in range(C):
                    last = mm(bank, lhs(c), rhs(c), start=(c == 0), stop=(c == C - 1 and more is None))
                return last

            def dense3(bank, lhs, rhs, more=False):
                for c in range(C):
                    for a, b in ((0, 0), (0, 1), (1, 0)):
                        last = mm(bank, lhs(a, c), rhs(b, c), start=(c == 0 and a == b),
                                  stop=(c == C - 1 and a == 1 and not more))
                return last

            def key_tile(r, rounds, free):
                i = r % 2
                pe.wait_ge(l_xt[r], rounds)
                after(pe, S["k_copied"], free)
                dense(gb[i][:], lambda c: xt_s[r][:, c, :], lambda c: wkv_s[:, c, :]).then_inc(S["ka_mm"], 1)

            def queries(count, bank):
                pe.wait_ge(S["xq_lo"], count)
                dense3(bank[:], lambda p, c: xq_s[p][:, c, :], lambda p, c: wq_s[p][:, c, :]).then_inc(S["q_mm"], 1)

            def queries_t(n, bank):
                pe.wait_ge(S["q_rot"], n)
                o = bank[:].rearrange("p (a v q t) -> p a q v t", a=2, v=2, q=2)
                for k in range(4):
                    last = nc.tensor.transpose(o[:, k // 2, k % 2], qrot[:, 128 * k:128 * k + 128], ident)
                last.then_inc(S["qt_mm"], 1)

            pe.wait_ge(l_xt[0], 16)
            for c in range(C):
                pe.wait_ge(l_wkv[c], 16)
                last = mm(gb[0][:], xt_s[0][:, c, :], wkv_s[:, c, :], start=(c == 0), stop=(c == C - 1))
            last.then_inc(S["ka_mm"], 1)
            for n in range(1, 4):
                key_tile(n, 16, n - 1)
            HW = WS * NB // 2
            pe.wait_ge(S["blkd_ready"], 1)
            pe.wait_ge(S["l_few"], 16)
            bd = blkd[:].rearrange("p s b -> p (s b)")
            for i in range(2):
                last = mm(ob[i][0:NB, 0:HW], con("ones", NB), bd[:, HW * i:HW * i + HW], start=True, stop=True)
            last.then_inc(S["blkrow_mm"], 1)
            for n in range(4, HALF_A):
                key_tile(n - 4, 32, n - 1)
            pe.wait_ge(S["later_ready"], 1)
            pe.wait_ge(S["covered"], 1)
            for j in range(NW):
                for k in range(NW):
                    last = mm(tb[0][0:NB, BLOCK * j:BLOCK * j + BLOCK], later[:, k, NB * j:NB * j + NB],
                              cover[:, BLOCK * k:BLOCK * k + BLOCK], start=(k == 0), stop=(k == NW - 1))
            last.then_inc(S["lose_mm"], 1)
            pe.wait_ge(S["wcode_ready"], 1)
            pe.wait_ge(S["blkrow_ev"], 2)
            for i in range(2):
                for j in range(NW):
                    last = mm(ob[i][0:BLOCK, 0:HW], wcode[:, BLOCK * j:BLOCK * j + BLOCK], same[:, j, HW * i:HW * i + HW],
                              start=(j == 0), stop=(j == NW - 1))
            last.then_inc(S["win_mm"], 1)
            pe.wait_ge(S["rows_ready"], 1)
            pe.wait_ge(S["rows0_ready"], 1)
            spread = con("spread", BLOCK).rearrange("p (s q) -> p s q", s=SP_)
            for k in range(2):
                src = rows[:, k, :].rearrange("p (c s b) -> p s c b", c=CH, s=SP_)
                for s in range(SP_):
                    last = mm(tb[0][0:KP, CH * NB * k:CH * NB * (k + 1)].rearrange("p (c b) -> p c b", c=CH),
                              spread[:, s, :], src[:, s], start=(s == 0), stop=(s == SP_ - 1))
            last.then_inc(S["idx_mm"], 1)
            pe.wait_ge(S["split_lo"], C)
            queries(1, sbk[0])

            with pe.Fori(HALF_A // 4, TILES // 4) as j:
                for r in range(4):
                    key_tile(r, j * 16 + 16, j * 4 + (r - 1))

            queries_t(1, sbk[1])
            pe.wait_ge(S["l_up"], 16 * (2 * C + 2))
            dense(tb[1][0:64, :], lambda c: a2_s[:, c, :], lambda c: wt_s[:, c, :]).then_inc(S["down_mm"], 1)
            dense(ob[0][0:64, :], lambda c: b2_s[:, c, :], lambda c: wpt_s[:, c, :]).then_inc(S["up_mm"], 1)
            pe.wait_ge(S["down_ev"], 1)
            for c in range(C):
                last = nc.tensor.transpose(ob[1][:, 64 * c:64 * c + 64], down_t[:, 128 * c:128 * c + 128], ident[0:64, 0:64])
            last.then_inc(S["downt_mm"], 1)

            def keys_t(t, u, k):
                r, done = t.ring(u + k)
                pe.wait_ge(kv_new[r], done)
                for p in range(2):
                    after(pe, S["pt_ev"], t.b(u, 4, 4 * (k - 2) + 3 + p))
                    for c in range(CH):
                        last = nc.tensor.transpose(tb[p][:, KP * c:KP * c + KP], kv_s[r][:, c, 128 * p:128 * p + 128],
                                                   ident[0:KP, 0:KP])
                    last.then_inc(S["kt_mm"], 1)

            def scores(t, u, k, heads):
                if (t.part(u) + k) % 2 == 0 and heads[0] == 0:
                    pe.wait_ge(S["qlo_ready"], t.n(2, 2 * ((u + k) // 2) + 2))
                for g in heads:
                    p, h = g // 2, g % 2
                    pe.wait_ge(S["kt_ev"], t.b(u, 4, 4 * k + g + 1))
                    after(pe, S["negs_ready"], t.b(u, 4, 4 * k + g - 1))
                    v = (u + k) % 2
                    cols = slice(256 * p + 128 * v, 256 * p + 128 * v + 128)
                    mm(sbk[g % 2][:, 0:WK], q_hi[h][:, cols], kt_s[g][:], start=True, stop=False)
                    mm(sbk[g % 2][:, 0:WK], q_lo[h][:, cols], kt_s[g][:], start=False, stop=True).then_inc(S["s_mm"], 1)

            def probs_t(t, u, g, last_batch):
                i = t.part(u) % 2
                if g >= 2:
                    pe.wait_ge(S["pt_ev"], t.b(u, 4, g - 1))
                elif last_batch:
                    pe.wait_ge(S["pt_ev"], t.b(u, 4, g - 1))
                else:
                    pe.wait_ge(S["kt_ev"], t.b(u, 4, 4 + 2 * g + 2))
                pe.wait_ge(S["prob_ready"], t.b(u, 4, g + 1))
                for c in range(CH):
                    last = nc.tensor.transpose(tb[g % 2][0:KP, 128 * c:128 * c + 128], prob[i][:, g, KP * c:KP * c + KP], ident)
                last.then_inc(S["pt_mm"], 1)

            def values(t, u, p):
                r, _ = t.ring(u)
                pe.wait_ge(S["pt_ev"], t.b(u, 4, 2 * p + 2))
                after(pe, S["ot_lo"], t.b(u, 1, -1))
                for c in range(CH):
                    for h in range(2):
                        g = 2 * p + h
                        last = mm(ob[u][64 * h:64 * h + 64, 128 * p:128 * p + 128], kv_s[r][:, c, 256 + 64 * g:320 + 64 * g],
                                  pt_s[g][:, c, :], start=(c == 0), stop=(c == CH - 1))
                last.then_inc(S["pv_mm"], 1)

            def project(t):
                pe.wait_ge(S["ot_lo"], t.b(0, 1, 0))
                dense3(gb[0][:], lambda p, c: ot_s[p][:, c, :], lambda p, c: wo_s[p][:, c, :]).then_inc(S["wo_mm"], 1)

            def layer1(t, queries_in_bank):
                pe.wait_ge(S["x1_ready"], t.n(1, 0))
                pe.wait_ge(S["w1i_ready"], t.n(1, 0))
                if queries_in_bank:
                    pe.wait_ge(S["qlo_ready"], t.n(2, 2))
                for c in range(C):
                    last = mm(gb[1][:, 128 * c:128 * c + 128], x1[:, 128 * c:128 * c + 128], w1i[:], start=True, stop=True)
                last.then_inc(S["l1_mm"], 1)

            def ranks2(t):
                pe.wait_ge(S["x2_ready"], t.n(1, 0))
                dense(ob[1][0:64, 0:128], lambda c: down2[:, c, :], lambda c: x2t[:, c, :]).then_inc(S["z2_mm"], 1)

            def layer2(t):
                for k in range(C):
                    o = gb[1][:, 128 * k:128 * k + 128]
                    dense(o, lambda c: wb_s[:, c, 128 * k:128 * k + 128], lambda c: x2t[:, c, :], more=True)
                    if k == 0:
                        pe.wait_ge(S["z2_ready"], t.n(1, 0))
                    last = mm(o, up2[:, 128 * k:128 * k + 128], z2m[:], start=False, stop=True)
                last.then_inc(S["x3_mm"], 1)

            def ranks3(t):
                pe.wait_ge(S["x3_ready"], t.n(1, 0))
                dense(ob[1][:, 0:128], lambda c: a3_s[:, c, :], lambda c: x3t[:, c, :]).then_inc(S["z3_mm"], 1)

            def layer3(t, queries_in_bank):
                if queries_in_bank:
                    pe.wait_ge(S["q_t2"], t.n(1, 2))
                pe.wait_ge(S["x3_lo"], t.n(1, 0))
                dense3(gb[0][:], lambda p, c: x3s[p][:, c, :], lambda p, c: w3_s[p][:, c, :], more=True)

            def layer3_ranks(t):
                pe.wait_ge(S["z3_ready"], t.n(1, 0))
                mm(gb[0][:], z3m[:], b3_s[:], start=False, stop=True).then_inc(S["out_mm"], 1)

            def tile(t, first, last):
                keys_t(t, 0, 1)
                if not first:
                    project(t)
                scores(t, 0, 1, (0, 1))
                probs_t(t, 0, 0, False)
                probs_t(t, 0, 1, False)
                scores(t, 0, 1, (2, 3))
                if not last:
                    if not first:
                        pe.wait_ge(S["x1_ready"], t.n(1, 0))
                    else:
                        pe.wait_ge(S["k_copied"], TILES)
                    queries(t.n(1, 2), gb[0])
                if not first:
                    layer1(t, True)
                values(t, 0, 0)
                probs_t(t, 0, 2, False)
                probs_t(t, 0, 3, False)
                if not first:
                    ranks2(t)
                    layer2(t)
                values(t, 0, 1)
                if not last:
                    keys_t(t, 1, 1)
                if not first:
                    ranks3(t)
                if not last:
                    queries_t(t.n(1, 2), gb[1])
                if not first:
                    layer3(t, not last)
                probs_t(t, 1, 0, last)
                probs_t(t, 1, 1, last)
                if not first:
                    layer3_ranks(t)
                values(t, 1, 0)
                probs_t(t, 1, 2, last)
                probs_t(t, 1, 3, last)
                if not last:
                    scores(t, 1, 1, (0, 1))
                values(t, 1, 1)
                if not last:
                    scores(t, 1, 1, (2, 3))

            pe.wait_ge(S["idx_ready"], 1)
            pe.wait_ge(S["downt_ev"], 1)
            pe.wait_ge(S["up_ev"], 1)
            pe.wait_ge(S["w_ident"], 1)
            pe.wait_ge(S["split_lo"], len(splits))
            pe.wait_ge(S["l_low3"], 32)
            keys_t(Tile(0, 0), 0, 0)
            scores(Tile(0, 0), 0, 0, range(G))
            tile(Tile(0, 0), True, False)
            with pe.Fori(0, TILES // 2 - 1) as j:
                for c in (1, 2):
                    tile(Tile(j, c), False, False)
            tile(Tile(TILES // 2 - 1, 1), False, True)
            end = Tile(TILES // 2, 0)
            project(end)
            layer1(end, False)
            ranks2(end)
            layer2(end)
            ranks3(end)
            layer3(end, False)
            layer3_ranks(end)


def kernel(x, itok_Bx257_0_4111, itok_B_37_3939, itok_B_0_7, itok_B_0_3, itok_B_0_6,
           L0_cond_Wq, L0_cond_Wk, L0_cond_Wv, L0_cond_Wo, L0_cond_q_norm_scale, L0_cond_k_norm_scale,
           L0_cond_k_blocks, L0_cond_v_blocks, L1_cond_weights, L2_cond_W_base, L2_cond_Wt, L2_cond_A,
           L2_cond_B_w, L2_cond_Wp, L2_cond_scaling, L3_cond_W, L3_cond_A, L3_cond_Bm, L3_cond_scalings):
    import concourse.bacc as bacc
    from concourse.bass_utils import run_bass_kernel_spmd

    def chunks(a):
        a = np.asarray(a)
        return np.ascontiguousarray(a.reshape(-1, 128, a.shape[1]).transpose(1, 0, 2))

    x = np.asarray(x)
    xf = x.reshape(TILES, 128, D)
    wq = np.asarray(L0_cond_Wq).T.reshape(D, 2, 2, 2, HD)
    wo = np.asarray(L0_cond_Wo).T.reshape(2, 2, 2, HD, D)
    rows = np.concatenate([np.asarray(a).transpose(0, 2, 1, 3).reshape(NPOOL * BLOCK, G * HD)
                           for a in (L0_cond_k_blocks, L0_cond_v_blocks)], axis=1)
    arrays = dict(
        xt=np.ascontiguousarray(xf.reshape(TILES, 128, C, 128).transpose(0, 3, 2, 1)),
        xtok=np.ascontiguousarray(xf),
        kvrows=rows,
        wkv=chunks(np.concatenate([np.asarray(L0_cond_Wk), np.asarray(L0_cond_Wv)], axis=0).T),
        wq=chunks(wq.transpose(0, 1, 3, 2, 4).reshape(D, 512)),
        wo=chunks(wo.transpose(0, 2, 1, 3, 4).reshape(512, D)),
        qs=np.asarray(L0_cond_q_norm_scale), ks=np.asarray(L0_cond_k_norm_scale),
        w1=np.asarray(L1_cond_weights),
        wb=chunks(np.asarray(L2_cond_W_base).T),
        wt=chunks(L2_cond_Wt),
        a2t=chunks(np.asarray(L2_cond_A).reshape(NE2 * RANK, D).T),
        b2t=chunks(np.asarray(L2_cond_B_w).transpose(1, 0, 2).reshape(D, NE2 * RANK)),
        wpt=chunks(np.asarray(L2_cond_Wp).T),
        s2=np.repeat(np.asarray(L2_cond_scaling), RANK)[:, None],
        w3=chunks(np.asarray(L3_cond_W).T),
        a3t=chunks(np.asarray(L3_cond_A).reshape(NE3 * RANK, D).T),
        b3t=np.ascontiguousarray(np.asarray(L3_cond_Bm).transpose(0, 2, 1).reshape(NE3 * RANK, D)),
        s3=np.repeat(np.asarray(L3_cond_scalings), RANK)[:, None],
        table=np.lib.stride_tricks.sliding_window_view(
            np.concatenate([np.zeros(WS - NW, np.int32), np.asarray(itok_Bx257_0_4111).reshape(-1)]), WS), kvl=np.asarray(itok_B_37_3939),
        subj=np.asarray(itok_B_0_7).reshape(TILES, 1, 2),
        ad2=np.asarray(itok_B_0_3), ad3=np.asarray(itok_B_0_6),
        const=constants()[0], constf=constants()[1],
    )
    arrays = {n: np.ascontiguousarray(a) for n, a in arrays.items()}
    nc = bacc.Bacc("TRN2", target_bir_lowering=False, num_devices=1)
    args = {n: nc.dram_tensor(n + "_dram", a.shape, mybir.dt.from_np(a.dtype), kind="ExternalInput").ap()
            for n, a in arrays.items()}
    out = nc.dram_tensor("out_dram", (TILES, 128, D), mybir.dt.float32, kind="ExternalOutput").ap()
    build(nc, out=out, **args)
    r = run_bass_kernel_spmd(nc, [{n + "_dram": a for n, a in arrays.items()}], core_ids=[0])
    return r.results[0]["out_dram"].reshape(NB, NT, D)
```
